# Optimizing a Trainium2 kernel written in Bass

```python
import numpy as np
import jax
import jax.numpy as jnp

def _softmax(x, axis=-1):
    return jax.nn.softmax(x, axis=axis)

def _gelu(x):
    return jax.nn.gelu(x, approximate=True)

def _silu(x):
    return jax.nn.silu(x)

def _sigmoid(x):
    return jax.nn.sigmoid(x)

def _layernorm(x, axis=-1, eps=1e-05):
    m = jnp.mean(x, axis=axis, keepdims=True)
    v = jnp.var(x, axis=axis, keepdims=True)
    return (x - m) / jnp.sqrt(v + eps)

def _scatter_add(tgt, idx, src, axis=0):
    return tgt.at[idx].add(src)

def _segment_sum(src, seg, n):
    return jax.ops.segment_sum(src, seg, n)
kernel_name = 'mk_gnn_preln_d2_gnn_r8_3f1610'

def setup_inputs(seed: int=0):
    np.random.seed(seed)
    _w = jnp.asarray

    def _rec_inputs():
        import jax
        import jax.numpy as jnp
        _gk = jax.random.key(seed)
        x = -0.0002117 + 1 * jax.random.normal(jax.random.fold_in(_gk, 1), (3125, 1024), jnp.float32)
        src = jax.random.randint(jax.random.fold_in(_gk, 2), (50000,), 0, 3125, jnp.int32)
        dst = jax.random.randint(jax.random.fold_in(_gk, 3), (50000,), 0, 3125, jnp.int32)
        _o = jnp.argsort(dst, stable=True)
        src = src[_o]
        dst = dst[_o]
        return (x, src, dst)
    x, src, dst = _rec_inputs()

    def _L0_gnn_setup():
        import jax, jax.numpy as jnp
        import numpy as np
        N = 3125
        E = 50000
        H = 4
        C = 256
        D_IN = 1024
        NEG_SLOPE = 0.2
        key = jax.random.key(seed)
        k1, k2, k3, k4, k5, k6 = jax.random.split(key, 6)
        x = jax.random.normal(k1, (N, D_IN), dtype=jnp.float32)
        edge_index = jax.random.randint(k2, (2, E), 0, N, dtype=jnp.int64)
        scale = 1.0 / np.sqrt(D_IN)
        W = jax.random.normal(k3, (D_IN, H * C), dtype=jnp.float32) * scale
        att_src = jax.random.normal(k4, (H, C), dtype=jnp.float32) * 0.1
        att_dst = jax.random.normal(k5, (H, C), dtype=jnp.float32) * 0.1
        bias = jax.random.normal(k6, (H * C,), dtype=jnp.float32) * 0.01
        return {'x': x, 'edge_index': edge_index, 'W': W, 'att_src': att_src, 'att_dst': att_dst, 'bias': bias}
    _L0_gnn_all = _L0_gnn_setup()
    _L0_gnn_in = {k: v for k, v in _L0_gnn_all.items() if k in ('W', 'att_src', 'att_dst', 'bias')}
    del _L0_gnn_all

    def _L1_gnn_setup():
        import jax, jax.numpy as jnp
        import numpy as np
        N_NODES = 3125
        N_EDGES = 50000
        D = 1024

        def _sage_layer(h, edge_src, edge_dst, deg_inv, W_self, W_neigh, b):
            msg = h[edge_src]
            agg = jax.ops.segment_sum(msg, edge_dst, num_segments=h.shape[0])
            mean = agg * deg_inv[:, None]
            return h @ W_self + mean @ W_neigh + b
        key = jax.random.key(seed)
        ks = jax.random.split(key, 8)
        s = 1.0 / np.sqrt(D)
        return {'x': jax.random.normal(ks[0], (N_NODES, D), dtype=jnp.float32), 'edge_src': jax.random.randint(ks[1], (N_EDGES,), 0, N_NODES, dtype=jnp.int32), 'edge_dst': jax.random.randint(ks[2], (N_EDGES,), 0, N_NODES, dtype=jnp.int32), 'W_self0': jax.random.normal(ks[3], (D, D), dtype=jnp.float32) * s, 'W_neigh0': jax.random.normal(ks[4], (D, D), dtype=jnp.float32) * s, 'b0': jnp.zeros((D,), dtype=jnp.float32), 'W_self1': jax.random.normal(ks[5], (D, D), dtype=jnp.float32) * s, 'W_neigh1': jax.random.normal(ks[6], (D, D), dtype=jnp.float32) * s, 'b1': jnp.zeros((D,), dtype=jnp.float32)}
    _L1_gnn_all = _L1_gnn_setup()
    _L1_gnn_in = {k: v for k, v in _L1_gnn_all.items() if k in ('W_self0', 'W_neigh0', 'b0', 'W_self1', 'W_neigh1', 'b1')}
    del _L1_gnn_all
    return {'x': x, 'src': src, 'dst': dst, 'L0_gnn_W': _L0_gnn_in['W'], 'L0_gnn_att_src': _L0_gnn_in['att_src'], 'L0_gnn_att_dst': _L0_gnn_in['att_dst'], 'L0_gnn_bias': _L0_gnn_in['bias'], 'L1_gnn_W_self0': _L1_gnn_in['W_self0'], 'L1_gnn_W_neigh0': _L1_gnn_in['W_neigh0'], 'L1_gnn_b0': _L1_gnn_in['b0'], 'L1_gnn_W_self1': _L1_gnn_in['W_self1'], 'L1_gnn_W_neigh1': _L1_gnn_in['W_neigh1'], 'L1_gnn_b1': _L1_gnn_in['b1']}

def reference(x, src, dst, L0_gnn_W, L0_gnn_att_src, L0_gnn_att_dst, L0_gnn_bias, L1_gnn_W_self0, L1_gnn_W_neigh0, L1_gnn_b0, L1_gnn_W_self1, L1_gnn_W_neigh1, L1_gnn_b1):
    import jax
    import jax.numpy as jnp

    def _L0_gnn_ref(x, edge_index, W, att_src, att_dst, bias):
        import jax, jax.numpy as jnp
        import numpy as np
        N = 3125
        E = 50000
        H = 4
        C = 256
        D_IN = 1024
        NEG_SLOPE = 0.2
        xp = (x @ W).reshape(N, H, C)
        a_src = jnp.einsum('nhc,hc->nh', xp, att_src)
        a_dst = jnp.einsum('nhc,hc->nh', xp, att_dst)
        loops = jnp.arange(N, dtype=edge_index.dtype)
        src = jnp.concatenate([edge_index[0], loops])
        dst = jnp.concatenate([edge_index[1], loops])
        e = jax.nn.leaky_relu(a_src[src] + a_dst[dst], NEG_SLOPE)
        m = jax.ops.segment_max(e, dst, num_segments=N)
        ee = jnp.exp(e - m[dst])
        z = jax.ops.segment_sum(ee, dst, num_segments=N)
        alpha = ee / z[dst]
        msgs = xp[src] * alpha[:, :, None]
        out = jax.ops.segment_sum(msgs, dst, num_segments=N)
        out = out.reshape(N, H * C) + bias
        return jax.nn.relu(out)

    def _L1_gnn_ref(x, edge_src, edge_dst, W_self0, W_neigh0, b0, W_self1, W_neigh1, b1):
        import jax, jax.numpy as jnp
        import numpy as np
        N_NODES = 3125
        N_EDGES = 50000
        D = 1024

        def _sage_layer(h, edge_src, edge_dst, deg_inv, W_self, W_neigh, b):
            msg = h[edge_src]
            agg = jax.ops.segment_sum(msg, edge_dst, num_segments=h.shape[0])
            mean = agg * deg_inv[:, None]
            return h @ W_self + mean @ W_neigh + b
        N = x.shape[0]
        deg = jax.ops.segment_sum(jnp.ones_like(edge_dst, dtype=x.dtype), edge_dst, num_segments=N)
        deg_inv = 1.0 / jnp.maximum(deg, 1.0)
        h = jax.nn.relu(_sage_layer(x, edge_src, edge_dst, deg_inv, W_self0, W_neigh0, b0))
        out = _sage_layer(h, edge_src, edge_dst, deg_inv, W_self1, W_neigh1, b1)
        return out
    edge_index = jnp.stack([src, dst])
    h = jnp.maximum(_layernorm(x, axis=-1), 0.0)
    x = x + _L0_gnn_ref(h, edge_index, L0_gnn_W, L0_gnn_att_src, L0_gnn_att_dst, L0_gnn_bias)
    h = jnp.maximum(_layernorm(x, axis=-1), 0.0)
    x = x + _L1_gnn_ref(h, src, dst, L1_gnn_W_self0, L1_gnn_W_neigh0, L1_gnn_b0, L1_gnn_W_self1, L1_gnn_W_neigh1, L1_gnn_b1)
    return x

_drawn_inputs = setup_inputs


def setup_inputs(seed=0):
    import zlib

    import numpy as np

    out = dict(_drawn_inputs(seed))
    spreads = {'L1_gnn_b0': (0.0, 0.1), 'L1_gnn_b1': (0.0, 0.1)}
    factors = {'L0_gnn_bias': 7.778}
    for name, (base, spread) in spreads.items():
        noise = np.random.default_rng([zlib.crc32(name.encode()), seed]).standard_normal(out[name].shape)
        drawn = base * np.exp(spread * noise) if base else spread * noise
        out[name] = jnp.asarray(drawn.astype(out[name].dtype))
    for name, factor in factors.items():
        out[name] = (out[name] * factor).astype(out[name].dtype)
    return out
```

```python
import concourse.bass as bass
from concourse import mybir
from contextlib import ExitStack


def bass_gat_sage_sage(nc, x_in, src_in, dst_in, w_gat, att_src, att_dst, gat_bias,
                       w_self0, w_neigh0, b0, w_self1, w_neigh1, b1, out):
    f32, f32r, i32 = mybir.dt.float32, mybir.dt.float32r, mybir.dt.int32
    ALU = mybir.AluOpType
    ACT = mybir.ActivationFunctionType
    X = mybir.AxisListType.X
    ds = bass.ds

    N, D = x_in.shape
    E = src_in.shape[0]
    H, C = att_src.shape
    P = 128
    TN = 125
    NT = N // TN
    CH = P
    CPP = 4
    EP = -(-E // (CPP * CH))
    NCH = EP * CPP
    NS = NCH + NT - 1
    SB = 4
    SP_ = NS // SB
    U = 4
    KT = D // P
    HALF = 512
    FAR = 8192.0
    BIG = 1.0e30
    EPS = 1e-5
    SLOPE = 0.2
    assert NT * TN == N and NT % 2 == 1 and SP_ * SB == NS and NS % (2 * U) == 0 and H * C == D

    def tiles(ap):
        return ap.rearrange("(t p) d -> p t d", p=TN)

    def scratch(name, shape, dt=f32):
        return nc.dram_tensor(name, shape, dt).ap()

    edge_rows = scratch("edge_rows", (NCH, 2 * CH), i32)
    xp_rows = scratch("xp_rows", (N, D))
    att_rows = scratch("att_rows", (N, H))
    x1_rows = scratch("x1_rows", (N, D))
    h_rows = scratch("h_rows", (N, D))
    part0_rows = scratch("part0_rows", (N, D))
    h1_rows = scratch("h1_rows", (N, D))
    part1_rows = scratch("part1_rows", (N, D))

    def opener(ctx, tag):
        def sb(name, shape, dt=f32):
            return ctx.enter_context(nc.sbuf_tensor(f"{tag}_{name}", shape, dt))

        def ps(name, shape, dt=f32):
            return ctx.enter_context(nc.psum_tensor(f"{tag}_{name}", shape, dt))

        sems = []

        def sem(name):
            sems.append(nc.alloc_semaphore(f"{tag}_{name}"))
            return sems[-1]

        def clear():
            if sems:
                nc.clear_and_free_semaphores(sems)
                nc.all_engine_barrier()
        ctx.callback(clear)
        return sb, ps, sem

    def chain(eng, sem, start=0):
        done = [0]

        def step(ins):
            done[0] += 1
            ins.then_inc(sem, 1)
            eng.wait_ge(sem, start + done[0])
        return step

    def each_tile(eng, front, back):
        front(0, 0, 0)
        front(1, 1, 0)
        back(0, 0, 0)
        with eng.Fori(0, (NT - 3) // 2) as j:
            for u in range(2):
                front(2 * j + (2 + u), u, j + 1)
                back(2 * j + (1 + u), (1 + u) % 2, j + (1 + u) // 2)
        front(NT - 1, 0, (NT - 1) // 2)
        back(NT - 2, 1, (NT - 2) // 2)
        back(NT - 1, 0, (NT - 1) // 2)

    top = ExitStack()
    with top:
        sb0, _, _ = opener(top, "all")
        ident = sb0("ident", [P, P])
        iota_tn = sb0("iota_tn", [P, TN])
        ones = sb0("ones", [P, P])
        idx = sb0("idx", [P, NS], i32)
        rel = sb0("rel", [P, NS])
        tile_of = sb0("tile_of", [1, NS], i32)
        deg_inv = sb0("deg_inv", [TN, NT])

        def tables():
            with ExitStack() as ctx:
                sb, ps, sem = opener(ctx, "tab")
                edges = sb("edges", [EP, CPP, 2, CH], i32)
                dst_f = sb("dst_f", [EP, CPP, CH])
                junk = sb("junk", [EP, CPP, CH])
                below = sb("below", [EP, NT - 1])
                start_i = sb("start_i", [P, NT - 1], i32)
                start_c = sb("start_c", [P, NT - 1])
                first = sb("first", [P, NT - 1])
                tile_no = sb("tile_no", [P, NT - 1])
                step_p = sb("step_p", [SP_, SB])
                step_r = sb("step_r", [1, NS])
                tile_r = sb("tile_r", [1, NS])
                junk2 = sb("junk2", [SP_, NT - 1])
                tile_p = sb("tile_p", [SP_, SB])
                lo_p = sb("lo_p", [SP_, SB])
                chunk_f = sb("chunk_f", [SP_, SB])
                chunk_i = sb("chunk_i", [SP_, SB], i32)
                got = sb("got", [SP_, SB, 2 * CH], i32)
                rel_p = sb("rel_p", [SP_, SB, CH])
                in_p = sb("in_p", [SP_, SB, CH])
                src_p = sb("src_p", [SP_, SB, CH])
                start_ps = ps("start_ps", [P, HALF])
                src_ps = ps("src_ps", [P, HALF])
                rel_ps = ps("rel_ps", [P, HALF])
                padded, loaded, stored = sem("padded"), sem("loaded"), sem("stored")
                made, counted, summed = sem("made"), sem("counted"), sem("summed")
                chunks_ready, rows_ready, turned = sem("chunks_ready"), sem("rows_ready"), sem("turned")
                fetched = [sem(f"fetched{b}") for b in range(SB)]
                v_step, g_step = sem("v_step"), sem("g_step")
                block = ctx.enter_context(nc.Block())
                whole = E // (CPP * CH)
                rest = E - whole * CPP * CH
                LOADS = 2 * (1 + -(-rest // CH))

                @block.sync
                def _(sp):
                    sp.wait_ge(padded, 1)
                    for k, ap in enumerate((src_in, dst_in)):
                        sp.dma_start(edges[0:whole, :, k, :],
                                     ap[0:whole * CPP * CH].rearrange("(p c e) -> p c e", c=CPP, e=CH)).then_inc(loaded, 16)
                        r = 0
                        for c in range(CPP):
                            n = min(CH, rest - r)
                            if n > 0:
                                sp.dma_start(edges[whole:whole + 1, c, k, 0:n],
                                             ap[whole * CPP * CH + r:whole * CPP * CH + r + n]
                                             .rearrange("(a n) -> a n", a=1)).then_inc(loaded, 16)
                                r += n
                    sp.wait_ge(loaded, LOADS * 16)
                    sp.dma_start(edge_rows.rearrange("(p c) e -> p (c e)", c=CPP),
                                 edges[:, :, :, :].rearrange("p c k e -> p (c k e)")).then_inc(stored, 16)
                    sp.wait_ge(stored, 16)

                @block.gpsimd
                def _(g):
                    step = chain(g, g_step)
                    g.iota(iota_tn[:, :], [[1, TN]], base=0, channel_multiplier=0,
                           allow_small_or_imprecise_dtypes=True)
                    g.iota(tile_no[:, :], [[1, NT - 1]], base=1, channel_multiplier=0,
                           allow_small_or_imprecise_dtypes=True)
                    g.iota(step_p[:, :], [[SP_, SB]], base=0, channel_multiplier=1,
                           allow_small_or_imprecise_dtypes=True)
                    g.iota(step_r[:, :], [[1, NS]], base=0, channel_multiplier=0,
                           allow_small_or_imprecise_dtypes=True)
                    step(g.memset(ident[:, :], 0.0))
                    g.affine_select(out=ident[:, :], in_=ident[:, :], compare_op=ALU.not_equal, fill=1.0,
                                    base=0, pattern=[[-1, P]], channel_multiplier=1).then_inc(made, 1)
                    g.wait_ge(chunks_ready, 1)
                    g.wait_ge(stored, 16)
                    for b in range(SB):
                        g.indirect_dma_start(
                            out=got[:, b, :], out_offset=None, in_=edge_rows[:, :],
                            in_offset=bass.IndirectOffsetOnAxis(ap=chunk_i[:, b:b + 1], axis=0)).then_inc(fetched[b], 16)
                    for b in range(SB):
                        g.wait_ge(fetched[b], 16)

                @block.vector
                def _(v):
                    step = chain(v, v_step)
                    v.memset(edges[:, :, :, :], int(FAR)).then_inc(padded, 1)
                    step(v.memset(ones[:, :], 1.0))
                    v.wait_ge(loaded, LOADS * 16)
                    step(v.tensor_copy(dst_f[:, :, :], edges[:, :, 1, :]))
                    for t in range(1, NT):
                        last = v.tensor_scalar(junk[:, :, :], dst_f[:, :, :], float(t * TN), 0.0,
                                               ALU.is_lt, ALU.add, accum_out=below[:, t - 1:t])
                        if t < NT - 1:
                            step(last)
                    last.then_inc(counted, 1)
                    v.wait_ge(summed, 1)
                    step(v.tensor_copy(start_i[:, :], start_ps[:, 0:NT - 1]))
                    step(v.tensor_scalar(start_i[:, :], start_i[:, :], 7, None, ALU.arith_shift_right))
                    step(v.tensor_copy(start_c[:, :], start_i[:, :]))
                    v.wait_ge(made, 1)
                    step(v.tensor_tensor(first[:, :], start_c[:, :], tile_no[:, :], ALU.add))
                    for b in range(SB):
                        step(v.tensor_scalar(junk2[:, :], first[0:SP_, :], step_p[:, b:b + 1], 0.0,
                                             ALU.is_le, ALU.add, accum_out=tile_p[:, b:b + 1]))
                    step(v.tensor_tensor(chunk_f[:, :], step_p[:, :], tile_p[:, :], ALU.subtract))
                    step(v.tensor_scalar(lo_p[:, :], tile_p[:, :], float(TN), None, ALU.mult))
                    v.tensor_copy(chunk_i[:, :], chunk_f[:, :]).then_inc(chunks_ready, 1)
                    step(v.tensor_scalar(tile_r[:, :], step_r[:, :], first[0:1, 0:1], None, ALU.is_ge))
                    for t in range(1, NT - 1):
                        step(v.scalar_tensor_tensor(tile_r[:, :], step_r[:, :], first[0:1, t:t + 1],
                                                    tile_r[:, :], ALU.is_ge, ALU.add))
                    step(v.tensor_copy(tile_of[:, :], tile_r[:, :]))
                    for b in range(SB):
                        v.wait_ge(fetched[b], 16)
                        step(v.tensor_scalar(rel_p[:, b, :], got[:, b, CH:2 * CH], lo_p[:, b:b + 1], None,
                                             ALU.subtract))
                        step(v.tensor_scalar(in_p[:, b, :], rel_p[:, b, :], 0.0, None, ALU.is_ge))
                        step(v.scalar_tensor_tensor(in_p[:, b, :], rel_p[:, b, :], float(TN), in_p[:, b, :],
                                                    ALU.is_lt, ALU.mult))
                        step(v.tensor_scalar(in_p[:, b, :], in_p[:, b, :], -FAR, FAR, ALU.mult, ALU.add))
                        v.tensor_tensor(src_p[:, b, :], got[:, b, 0:CH], in_p[:, b, :], ALU.add).then_inc(rows_ready, 1)
                    v.wait_ge(turned, 1)
                    v.tensor_copy(idx[:, :], src_ps[:, 0:NS])
                    v.tensor_copy(rel[:, :], rel_ps[:, 0:NS])

                @block.tensor
                def _(t):
                    t.wait_ge(counted, 1)
                    t.matmul(start_ps[:, 0:NT - 1], ones[0:EP, :], below[:, :], start=True, stop=True).then_inc(summed, 1)
                    t.wait_ge(made, 1)
                    for b in range(SB):
                        t.wait_ge(rows_ready, b + 1)
                        t.transpose(src_ps[:, b * SP_:(b + 1) * SP_], src_p[:, b, :], ident[0:SP_, 0:SP_])
                        last = t.transpose(rel_ps[:, b * SP_:(b + 1) * SP_], rel_p[:, b, :], ident[0:SP_, 0:SP_])
                    last.then_inc(turned, 1)

        def project(tag, w, rows_in, rows_out, norm=False, bias=None, add=None, relu=False,
                    acc=None, att=None):
            with ExitStack() as ctx:
                sb, ps, sem = opener(ctx, tag)
                w_hi = sb("w_hi", [P, KT, D], f32r)
                w_lo = sb("w_lo", [P, KT, D], f32r)
                rows = sb("rows", [P, 2, D])
                a_hi = [sb(f"a_hi{i}", [P, KT, TN], f32r) for i in range(2)]
                a_lo = [sb(f"a_lo{i}", [P, KT, TN], f32r) for i in range(2)]
                if acc is None:
                    x_sb = sb("x_sb", [TN, 2, D])
                if acc is not None or norm:
                    hn = sb("hn", [TN, D])
                if norm:
                    stats = sb("stats", [TN, 2, 6])
                    mv = sb("mv", [TN, 2])
                    rstd = sb("rstd", [TN, 1])
                    shift = sb("shift", [TN, 1])
                if bias is not None:
                    bias_sb = sb("bias_sb", [TN, D])
                if att is not None:
                    att_sb = sb("att_sb", [P, 2, D])
                    tmp = sb("tmp", [P, D])
                    w_att = sb("w_att", [P, KT, 2 * H])
                    w_att_hi = sb("w_att_hi", [P, KT, 2 * H], f32r)
                    w_att_lo = sb("w_att_lo", [P, KT, 2 * H], f32r)
                    att_ps = ps("att_ps", [TN, HALF])
                turn_ps = ps("turn_ps", [P, 2, HALF])
                out_ps = [ps(f"out_ps{i}", [TN, 2, HALF]) for i in range(2)]
                w_loaded = [sem(f"w_loaded{i}") for i in range(2)]
                w_hi_done, w_lo_done, const_loaded = sem("w_hi_done"), sem("w_lo_done"), sem("const_loaded")
                x_loaded = [sem(f"x_loaded{i}") for i in range(2)]
                add_loaded = [sem(f"add_loaded{i}") for i in range(2)]
                stored = [sem(f"stored{i}") for i in range(2)]
                var_ready, std_ready, norm_ready = sem("var_ready"), sem("std_ready"), sem("norm_ready")
                a_ready, turned, hi_done, lo_done = sem("a_ready"), sem("turned"), sem("hi_done"), sem("lo_done")
                mm_done, out_ready = sem("mm_done"), sem("out_ready")
                att_done, v_step, summed = sem("att_done"), sem("v_step"), sem("summed")
                stats_ready = sem("stats_ready")
                block = ctx.enter_context(nc.Block())
                turn_v = turn_ps[:, :, 0:4 * TN].rearrange("p b (k n) -> p b k n", k=4)

                @block.sync
                def _(sp):
                    if bias is not None:
                        sp.dma_start(bias_sb[:, :], bias.partition_broadcast(TN)).then_inc(const_loaded, 16)
                    if att is not None:
                        for k in range(2):
                            sp.dma_start(att_sb[:, k, :], att[k].rearrange("h c -> (h c)").partition_broadcast(P)).then_inc(const_loaded, 16)
                    w_v = w.rearrange("(k p) n -> p k n", p=P)
                    for k in range(KT):
                        if k >= 2:
                            sp.wait_ge(w_lo_done, k - 1)
                        sp.dma_start(rows[:, k % 2:k % 2 + 1, :], w_v[:, k:k + 1, :]).then_inc(w_loaded[k % 2], 16)
                    if add is not None:
                        sp.wait_ge(w_lo_done, KT)

                    def front(m, slot, half):
                        if acc is None:
                            if not (type(m) is int and m < 2):
                                sp.wait_ge(a_ready if norm else lo_done, m - 1)
                            sp.dma_start(x_sb[:, slot:slot + 1, :], tiles(rows_in)[:, ds(m, 1), :]).then_inc(x_loaded[slot], 16)
                        if add is not None:
                            if not (type(m) is int and m < 2):
                                sp.wait_ge(stored[slot], 16 * half)
                            sp.dma_start(rows[0:TN, slot:slot + 1, :], tiles(add)[:, ds(m, 1), :]).then_inc(add_loaded[slot], 16)

                    def back(n, slot, half):
                        sp.wait_ge(out_ready, n + 1)
                        sp.dma_start(tiles(rows_out)[:, ds(n, 1), :], rows[0:TN, slot:slot + 1, :]).then_inc(stored[slot], 16)

                    each_tile(sp, front, back)
                    sp.wait_ge(stored[0], 16 * ((NT + 1) // 2))
                    sp.wait_ge(stored[1], 16 * (NT // 2))
                    if att is not None:
                        sp.wait_ge(att_done, NT)
                        sp.dma_start(tiles(att_rows), att_n[:, :, 0:H]).then_inc(const_loaded, 16)
                        sp.wait_ge(const_loaded, 48)

                @block.scalar
                def _(a):
                    for k in range(KT):
                        a.wait_ge(w_loaded[k % 2], 16 * (k // 2 + 1))
                        a.activation(w_hi[:, k, :], rows[:, k % 2, :], ACT.Copy).then_inc(w_hi_done, 1)

                    def front(m, slot, half):
                        if norm:
                            a.wait_ge(var_ready, m + 1)
                            a.activation(rstd[:, :], mv[:, 1:2], ACT.Sqrt).then_inc(std_ready, 1)
                            a.wait_ge(norm_ready, m + 1)
                            if not (type(m) is int and m < 1):
                                a.wait_ge(turned, m)
                            a.activation(hn[:, :], x_sb[:, slot, :], ACT.Relu, bias=shift[:, 0:1],
                                         scale=rstd[:, 0:1]).then_inc(a_ready, 1)
                        elif acc is not None:
                            if not (type(m) is int and m < 1):
                                a.wait_ge(turned, m)
                            a.activation(hn[:, :].rearrange("p (a d) -> p a d", a=1), acc[:, ds(m, 1), :], ACT.Copy,
                                         scale=deg_inv[:, ds(m, 1)]).then_inc(a_ready, 1)
                        a.wait_ge(turned, m + 1)
                        if not (type(m) is int and m < 2):
                            a.wait_ge(mm_done, m - 1)
                        for q in range(2):
                            last = a.activation(a_hi[slot][:, 4 * q:4 * q + 4, :], turn_v[:, q], ACT.Copy)
                        last.then_inc(hi_done, 1)

                    def back(n, slot, half):
                        if relu:
                            a.wait_ge(summed, n + 1)
                            a.activation(rows[0:TN, slot, :], rows[0:TN, slot, :], ACT.Relu).then_inc(out_ready, 1)

                    each_tile(a, front, back)

                @block.vector
                def _(v):
                    pre = chain(v, v_step)
                    if bias is not None:
                        v.wait_ge(const_loaded, 16)
                    if att is not None:
                        v.wait_ge(const_loaded, 32)
                    for k in range(KT):
                        v.wait_ge(w_loaded[k % 2], 16 * (k // 2 + 1))
                        if att is not None:
                            for q in range(2):
                                pre(v.tensor_tensor(tmp[:, :], rows[:, k % 2, :], att_sb[:, q, :], ALU.mult))
                                pre(v.tensor_reduce(w_att[:, k, q * H:(q + 1) * H], tmp[:, :].rearrange("p (h c) -> p h c", h=H),
                                                    axis=X, op=ALU.add))
                        v.wait_ge(w_hi_done, k + 1)
                        v.tensor_tensor(w_lo[:, k, :], rows[:, k % 2, :], w_hi[:, k, :].bitcast(f32), ALU.subtract).then_inc(w_lo_done, 1)
                    if att is not None:
                        pre(v.tensor_copy(w_att_hi[:, :, :], w_att[:, :, :]))
                        v.tensor_tensor(w_att_lo[:, :, :], w_att[:, :, :], w_att_hi[:, :, :].bitcast(f32), ALU.subtract).then_inc(w_lo_done, 1)
                    base = 4 * KT + 1 if att is not None else 0

                    def front(m, slot, half):
                        if norm:
                            PER = 5
                            step = chain(v, v_step, base + PER * m)
                            v.wait_ge(x_loaded[slot], 16 * (half + 1))
                            if not (type(m) is int and m < 1):
                                v.wait_ge(a_ready, m)
                            for q in range(2):
                                step(v.bn_stats(stats[:, q, :], x_sb[:, slot, q * HALF:(q + 1) * HALF]))
                            v.sem_inc(stats_ready, 1)
                            step(v.bn_aggr(mv[:, :], stats[:, :, :].rearrange("p a b -> p (a b)")))
                            v.tensor_scalar(mv[:, 1:2], mv[:, 1:2], EPS, None, ALU.add).then_inc(var_ready, 1)
                            v.wait_ge(std_ready, m + 1)
                            step(v.reciprocal(rstd[:, :], rstd[:, :]))
                            step(v.tensor_scalar(shift[:, :], mv[:, 0:1], -1.0, rstd[:, 0:1], ALU.mult, ALU.mult))
                            v.sem_inc(norm_ready, 1)
                        v.wait_ge(hi_done, m + 1)
                        if not (type(m) is int and m < 2):
                            v.wait_ge(mm_done, m - 1)
                        for q in range(2):
                            last = v.tensor_tensor(a_lo[slot][:, 4 * q:4 * q + 4, :], turn_v[:, q],
                                                   a_hi[slot][:, 4 * q:4 * q + 4, :].bitcast(f32), ALU.subtract)
                        last.then_inc(lo_done, 1)

                    def back(n, slot, half):
                        v.wait_ge(mm_done, n + 1)
                        if att is not None:
                            v.tensor_copy(att_n[:, ds(n, 1), :], att_ps[:, 0:2 * H].rearrange("p (a k) -> p a k", a=1)).then_inc(att_done, 1)
                        ro = rows[0:TN, slot, :]
                        po = out_ps[slot][:, :, :].rearrange("p a b -> p (a b)")
                        if add is not None:
                            v.wait_ge(add_loaded[slot], 16 * (half + 1))
                        elif type(n) is int and n < 2:
                            v.wait_ge(w_lo_done, KT)
                        else:
                            v.wait_ge(stored[slot], 16 * half)
                        if add is not None and bias is not None:
                            s2 = chain(v, summed, n)
                            s2(v.tensor_tensor(ro, po, ro, ALU.add))
                            v.tensor_tensor(ro, ro, bias_sb[:, :], ALU.add).then_inc(out_ready, 1)
                        else:
                            if add is not None:
                                last = v.tensor_tensor(ro, po, ro, ALU.add)
                            elif bias is not None:
                                last = v.tensor_tensor(ro, po, bias_sb[:, :], ALU.add)
                            else:
                                last = v.tensor_copy(ro, po)
                            last.then_inc(summed if relu else out_ready, 1)

                    each_tile(v, front, back)

                freed = summed if (relu or (add is not None and bias is not None)) else out_ready

                @block.tensor
                def _(t):
                    t.wait_ge(w_hi_done, KT)
                    t.wait_ge(w_lo_done, KT + (att is not None))

                    def front(m, slot, half):
                        if norm or acc is not None:
                            t.wait_ge(a_ready, m + 1)
                            src = hn[:, :]
                        else:
                            t.wait_ge(x_loaded[slot], 16 * (half + 1))
                            src = x_sb[:, slot, :]
                        if not (type(m) is int and m < 1):
                            t.wait_ge(lo_done, m)
                        for k in range(KT):
                            last = t.transpose(turn_v[:, k // 4, k % 4, :], src[:, k * P:(k + 1) * P], ident[0:TN, 0:TN])
                        last.then_inc(turned, 1)

                    def back(n, slot, half):
                        t.wait_ge(lo_done, n + 1)
                        if not (type(n) is int and n < 2):
                            t.wait_ge(freed, n - 1)
                        if att is not None:
                            if not (type(n) is int and n < 1):
                                t.wait_ge(att_done, n)
                        for k in range(KT):
                            parts = ((a_hi, w_hi), (a_hi, w_lo), (a_lo, w_hi))
                            for i, (a_, w_) in enumerate(parts):
                                first, last_ = (k == 0 and i == 0), (k == KT - 1 and i == 2)
                                for q in range(2):
                                    last = t.matmul(out_ps[slot][:, q, :], a_[slot][:, k, :], w_[:, k, q * HALF:(q + 1) * HALF],
                                                    start=first, stop=last_)
                                if att is not None:
                                    wa = w_att_hi if w_ is w_hi else w_att_lo
                                    last = t.matmul(att_ps[:, 0:2 * H], a_[slot][:, k, :], wa[:, k, :], start=first, stop=last_)
                        last.then_inc(mm_done, 1)

                    each_tile(t, front, back)

        def attention_max():
            with ExitStack() as ctx:
                sb, ps, sem = opener(ctx, "max")
                idx_now = sb("idx_now", [P, 2, U], i32)
                fetched = sb("fetched", [P, 2, U, H])
                away = sb("away", [P, 2, U, TN])
                cand = sb("cand", [P, U, H, TN])
                top_s = sb("top_s", [TN, U, H])
                cand_ps = [ps(f"cand_ps{k}", [TN, H, P]) for k in range(U)]
                idx_ready, cleared = sem("idx_ready"), sem("cleared")
                arrived = [[sem(f"arrived{s}{k}") for k in range(U)] for s in range(2)]
                cand_ready, turned, v_step, used = sem("cand_ready"), sem("turned"), sem("v_step"), sem("used")
                reduced, issuing = sem("reduced"), sem("issuing")
                block = ctx.enter_context(nc.Block())

                @block.gpsimd
                def _(g):
                    last_row = g.to_reg(N - 1)
                    with g.Fori(0, NS // (2 * U)) as i:
                        for s in range(2):
                            g.wait_ge(used, 2 * i + (s + 1))
                            g.tensor_copy(idx_now[:, s, :], idx[:, ds(2 * U * i + U * s, U)]).then_inc(idx_ready, 1)
                            g.wait_ge(idx_ready, 2 * i + (s + 1))
                            g.sem_inc(issuing, 1)
                            for k in range(U):
                                g.indirect_dma_start(
                                    out=fetched[:, s, k, :], out_offset=None, in_=att_rows[:, :],
                                    in_offset=bass.IndirectOffsetOnAxis(ap=idx_now[:, s, k:k + 1], axis=0),
                                    bounds_check=last_row, oob_is_err=False).then_inc(arrived[s][k], 16)

                @block.vector
                def _(v):
                    first = chain(v, cleared)
                    first(v.memset(fetched[:, :, :, :], 0.0))
                    first(v.tensor_copy(top_n[:, :, :], att_n[:, :, 0:H]))
                    v.sem_inc(used, 2)
                    PER = 1 + 2 * U + U
                    with v.Fori(0, NS // (2 * U)) as i:
                        tile = [v.value_load(tile_of[0:1, ds(2 * U * i + q, 1)], min_val=0, max_val=NT - 1) for q in range(2 * U)]
                        for s in range(2):
                            step = chain(v, v_step, (2 * i + s) * (1 + U))
                            step(v.tensor_tensor(away[:, s], iota_tn[:, :].unsqueeze(1).to_broadcast([P, U, TN]),
                                                 rel[:, ds(2 * U * i + U * s, U)].unsqueeze(2).to_broadcast([P, U, TN]), ALU.not_equal))
                            v.wait_ge(turned, (2 * i + s) * U)
                            for k in range(U):
                                v.wait_ge(arrived[s][k], 16 * (i + 1))
                                v.tensor_copy(att_e[:, ds(2 * U * i + (U * s + k), 1), :], fetched[:, s, k:k + 1, :])
                                last = v.scalar_tensor_tensor(
                                    cand[:, k], away[:, s, k:k + 1, :].to_broadcast([P, H, TN]), -BIG,
                                    fetched[:, s, k, :].unsqueeze(2).to_broadcast([P, H, TN]), ALU.mult, ALU.add)
                                last.then_inc(cand_ready, 1)
                            v.wait_ge(cand_ready, (2 * i + s + 1) * U)
                            v.sem_inc(used, 1)
                            for k in range(U):
                                v.wait_ge(turned, (2 * i + s) * U + (k + 1))
                                v.tensor_reduce(top_s[:, k, :], cand_ps[k][:, :, :], axis=X, op=ALU.max).then_inc(reduced, 1)
                            for k in range(U):
                                v.wait_ge(reduced, (2 * i + s) * U + (k + 1))
                                tl = ds(tile[U * s + k], 1)
                                step(v.tensor_tensor(top_n[:, tl, :], top_n[:, tl, :], top_s[:, k:k + 1, :], ALU.max))

                @block.tensor
                def _(t):
                    with t.Fori(0, NS // U) as i:
                        for k in range(U):
                            t.wait_ge(cand_ready, U * i + (k + 1))
                            if k == 0:
                                t.wait_ge(reduced, U * i)
                            for h in range(H):
                                last = t.transpose(cand_ps[k][:, h, :], cand[:, k, h, :], ident[:, :])
                            last.then_inc(turned, 1)

        def edge_weights():
            with ExitStack() as ctx:
                sb, ps, sem = opener(ctx, "wts")
                score_n = sb("score_n", [TN, NT, 2 * H])
                flat = sb("flat", [TN, NT, H])
                hot = sb("hot", [P, 2, U, TN])
                hot_t = sb("hot_t", [TN, 2, U, P])
                node_e = sb("node_e", [P, NS, 2 * H])
                raw = sb("raw", [P, NS, H])
                flat_e = sb("flat_e", [P, NS, H])
                hot_ps = [ps(f"hot_ps{i}", [TN, U, P]) for i in range(2)]
                node_ps = [ps(f"node_ps{i}", [P, U, 2 * H]) for i in range(2)]
                ready, hot_ready, turned, moved = sem("ready"), sem("hot_ready"), sem("turned"), sem("moved")
                spread, kept, v_step, raw_ready, own_ready = sem("spread"), sem("kept"), sem("v_step"), sem("raw_ready"), sem("own_ready")
                done = sem("done")
                block = ctx.enter_context(nc.Block())
                G = NS // U

                @block.vector
                def _(v):
                    step = chain(v, v_step)

                    def leaky(out_, in_, tmp_):
                        step(v.tensor_scalar(tmp_, in_, SLOPE, None, ALU.mult))
                        step(v.tensor_tensor(out_, in_, tmp_, ALU.max))
                    step(v.tensor_copy(score_n[:, :, H:2 * H], att_n[:, :, H:2 * H]))
                    step(v.tensor_tensor(top_n[:, :, :], top_n[:, :, :], att_n[:, :, H:2 * H], ALU.add))
                    leaky(score_n[:, :, 0:H], top_n[:, :, :], flat[:, :, :])
                    step(v.tensor_tensor(own_n[:, :, :], att_n[:, :, 0:H], att_n[:, :, H:2 * H], ALU.add))
                    leaky(own_n[:, :, :], own_n[:, :, :], flat[:, :, :])
                    step(v.tensor_tensor(own_n[:, :, :], own_n[:, :, :], score_n[:, :, 0:H], ALU.subtract))
                    v.sem_inc(ready, 1)
                    with v.Fori(0, G // 2) as i:
                        for s in range(2):
                            v.wait_ge(kept, 2 * i)
                            v.tensor_tensor(hot[:, s], iota_tn[:, :].unsqueeze(1).to_broadcast([P, U, TN]),
                                            rel[:, ds(2 * U * i + U * s, U)].unsqueeze(2).to_broadcast([P, U, TN]),
                                            ALU.is_equal).then_inc(hot_ready, 1)
                        for s in range(2):
                            v.wait_ge(spread, 2 * i + (s + 1))
                            v.tensor_copy(node_e[:, ds(2 * U * i + U * s, U), :], node_ps[s][:, :, :]).then_inc(kept, 1)
                    v.wait_ge(kept, G)
                    step(v.tensor_tensor(raw[:, :, :], att_e[:, :, :], node_e[:, :, H:2 * H], ALU.add))
                    leaky(raw[:, :, :], raw[:, :, :], flat_e[:, :, :])
                    step(v.tensor_tensor(raw[:, :, :], raw[:, :, :], node_e[:, :, 0:H], ALU.subtract))
                    step(v.tensor_scalar(raw[:, :, :], raw[:, :, :], 0.0, None, ALU.min))
                    v.memset(weight_e[:, :, H:H + 1], 1.0)
                    v.sem_inc(raw_ready, 1)

                @block.scalar
                def _(a):
                    with a.Fori(0, G // 2) as i:
                        for s in range(2):
                            a.wait_ge(turned, 2 * i + (s + 1))
                            a.wait_ge(spread, 2 * i)
                            a.activation(hot_t[:, s], hot_ps[s][:, :, :], ACT.Copy).then_inc(moved, 1)
                    a.wait_ge(ready, 1)
                    a.activation(own_n[:, :, :], own_n[:, :, :], ACT.Exp)
                    a.wait_ge(raw_ready, 1)
                    a.activation(weight_e[:, :, 0:H], raw[:, :, :], ACT.Exp)

                @block.tensor
                def _(t):
                    t.wait_ge(ready, 1)
                    with t.Fori(0, G // 2) as i:
                        tile = [t.value_load(tile_of[0:1, ds(2 * U * i + q, 1)], min_val=0, max_val=NT - 1) for q in range(2 * U)]
                        for s in range(2):
                            t.wait_ge(hot_ready, 2 * i + (s + 1))
                            t.wait_ge(moved, 2 * i)
                            for k in range(U):
                                last = t.transpose(hot_ps[s][:, k, :], hot[:, s, k, :], ident[:, :])
                            last.then_inc(turned, 1)
                        for s in range(2):
                            t.wait_ge(moved, 2 * i + (s + 1))
                            t.wait_ge(kept, 2 * i)
                            for k in range(U):
                                last = t.matmul(node_ps[s][:, k, :], hot_t[:, s, k, :], score_n[:, ds(tile[U * s + k], 1), :],
                                                start=True, stop=True)
                            last.then_inc(spread, 1)

        def aggregate(tag, rows_in, acc, acc_x=None):
            with ExitStack() as ctx:
                sb, ps, sem = opener(ctx, tag)
                weighted = acc_x is not None
                idx_now = sb("idx_now", [P, 2, U], i32)
                got = sb("got", [P, U, D])
                hot = sb("hot", [P, 2, TN])
                if weighted:
                    hot_w = sb("hot_w", [P, 2, H, TN])
                    extra_ps = [ps(f"extra_ps{i}", [TN, HALF]) for i in range(2)]
                sum_ps = [ps(f"sum_ps{i}", [TN, D]) for i in range(2)]
                idx_ready, hot_ready, hot_w_ready = sem("idx_ready"), sem("hot_ready"), sem("hot_w_ready")
                arrived = [sem(f"arrived{k}") for k in range(U)]
                issuing = sem("issuing")
                mm_done = sem("mm_done")
                added = sem("added")
                block = ctx.enter_context(nc.Block())
                rounds = NS // (2 * U)

                @block.gpsimd
                def _(g):
                    last_row = g.to_reg(N - 1)
                    with g.Fori(0, rounds) as i:
                        for s in range(2):
                            g.wait_ge(mm_done, 2 * U * i + (U * s + 1))
                            g.tensor_copy(idx_now[:, s, :], idx[:, ds(2 * U * i + U * s, U)]).then_inc(idx_ready, 1)
                            g.wait_ge(idx_ready, 2 * i + (s + 1))
                            g.sem_inc(issuing, 1)
                            for k in range(U):
                                g.wait_ge(mm_done, 2 * U * i + (U * s + k + 1))
                                g.sem_inc(issuing, 1)
                                g.indirect_dma_start(
                                    out=got[:, k, :], out_offset=None, in_=rows_in[:, :],
                                    in_offset=bass.IndirectOffsetOnAxis(ap=idx_now[:, s, k:k + 1], axis=0),
                                    bounds_check=last_row, oob_is_err=False).then_inc(arrived[k], 16)

                @block.vector
                def _(v):
                    v.memset(acc[:, :, :], 0.0)
                    if weighted:
                        v.memset(acc_x[:, :, :], 0.0)
                    v.memset(got[:, :, :], 0.0)
                    v.drain()
                    v.sem_inc(mm_done, U)
                    v.sem_inc(added, 2)

                    def make_hot(s, u):
                        v.wait_ge(mm_done, s + (U - 1) if not (type(s) is int) else s + (U - 1))
                        v.tensor_scalar(hot[:, u % 2, :], iota_tn[:, :], rel[:, ds(s, 1)], None, ALU.is_equal).then_inc(hot_ready, 1)

                    with v.Fori(0, rounds) as i:
                        tile = [v.value_load(tile_of[0:1, ds(2 * U * i + q, 1)], min_val=0, max_val=NT - 1) for q in range(2 * U)]
                        for u in range(2 * U):
                            s = 2 * U * i + u
                            if u == 0:
                                make_hot(s, 0)
                            if u < 2 * U - 1:
                                make_hot(s + 1, u + 1)
                            v.wait_ge(mm_done, s + (U + 1))
                            v.wait_ge(added, s + 2)
                            tl = ds(tile[u], 1)
                            if weighted:
                                v.tensor_tensor(acc_x[:, tl, :], extra_ps[u % 2][:, 0:H + 1].rearrange("p (a k) -> p a k", a=1),
                                                acc_x[:, tl, :], ALU.add)
                            v.tensor_tensor(acc[:, tl, :], sum_ps[u % 2][:, :].rearrange("p (a d) -> p a d", a=1),
                                            acc[:, tl, :], ALU.add).then_inc(added, 1)
                    if weighted:
                        v.wait_ge(added, NS + 2)
                        fin = chain(v, added, NS + 2)
                        fin(v.tensor_scalar(deg_inv[:, :], acc_x[:, :, H], 1.0, None, ALU.max))
                        fin(v.reciprocal(deg_inv[:, :], deg_inv[:, :]))

                if weighted:
                    @block.scalar
                    def _(a):
                        with a.Fori(0, rounds) as i:
                            for u in range(2 * U):
                                s = 2 * U * i + u
                                a.wait_ge(hot_ready, s + 1)
                                a.wait_ge(mm_done, s + (U - 1))
                                for h in range(H):
                                    last = a.activation(hot_w[:, u % 2, h, :], hot[:, u % 2, :], ACT.Copy,
                                                        scale=weight_e[:, ds(s, 1), h])
                                last.then_inc(hot_w_ready, 1)

                @block.tensor
                def _(t):
                    with t.Fori(0, rounds) as i:
                        for u in range(2 * U):
                            s = 2 * U * i + u
                            t.wait_ge(arrived[u % U], 16 * (2 * i + (u // U + 1)))
                            t.wait_ge(hot_w_ready if weighted else hot_ready, s + 1)
                            t.wait_ge(added, s + 1)
                            if weighted:
                                for h in range(H):
                                    t.matmul(sum_ps[u % 2][:, h * C:(h + 1) * C], hot_w[:, u % 2, h, :],
                                             got[:, u % U, h * C:(h + 1) * C], start=True, stop=True)
                                last = t.matmul(extra_ps[u % 2][:, 0:H + 1], hot[:, u % 2, :], weight_e[:, ds(s, 1), :],
                                                start=True, stop=True)
                            else:
                                for q in range(2):
                                    last = t.matmul(sum_ps[u % 2][:, q * HALF:(q + 1) * HALF], hot[:, u % 2, :],
                                                    got[:, u % U, q * HALF:(q + 1) * HALF], start=True, stop=True)
                            last.then_inc(mm_done, 1)

        def gat_finish(acc, acc_x):
            with ExitStack() as ctx:
                sb, ps, sem = opener(ctx, "fin")
                x_sb = sb("x_sb", [TN, 2, D])
                xp_sb = sb("xp_sb", [TN, 2, D])
                bias_sb = sb("bias_sb", [TN, D])
                val = sb("val", [TN, 2, D])
                h_sb = sb("h_sb", [TN, 2, D])
                z = sb("z", [TN, NT, H])
                stats = sb("stats", [TN, 2, 6])
                mv = sb("mv", [TN, 2])
                rstd = sb("rstd", [TN, 1])
                shift = sb("shift", [TN, 1])
                bias_in, stats_ready = sem("bias_in"), sem("stats_ready")
                x_loaded = [sem(f"x_loaded{i}") for i in range(2)]
                stored = [sem(f"stored{i}") for i in range(2)]
                v_step, val_ready, relu_done, x1_ready = sem("v_step"), sem("val_ready"), sem("relu_done"), sem("x1_ready")
                std_ready, norm_ready, h_ready = sem("std_ready"), sem("norm_ready"), sem("h_ready")
                block = ctx.enter_context(nc.Block())

                def no_step(*_):
                    pass

                @block.sync
                def _(sp):
                    sp.dma_start(bias_sb[:, :], gat_bias.partition_broadcast(TN)).then_inc(bias_in, 16)

                    def front(m, slot, half):
                        if not (type(m) is int and m < 2):
                            sp.wait_ge(h_ready, m - 1)
                        sp.dma_start(x_sb[:, slot:slot + 1, :], tiles(x_in)[:, ds(m, 1), :]).then_inc(x_loaded[slot], 16)
                        sp.dma_start(xp_sb[:, slot:slot + 1, :], tiles(xp_rows)[:, ds(m, 1), :]).then_inc(x_loaded[slot], 16)

                    def back(n, slot, half):
                        sp.wait_ge(x1_ready, n + 1)
                        sp.dma_start(tiles(x1_rows)[:, ds(n, 1), :], val[:, slot:slot + 1, :]).then_inc(stored[slot], 16)
                        sp.wait_ge(h_ready, n + 1)
                        sp.dma_start(tiles(h_rows)[:, ds(n, 1), :], h_sb[:, slot:slot + 1, :]).then_inc(stored[slot], 16)

                    each_tile(sp, front, back)
                    sp.wait_ge(stored[0], 32 * ((NT + 1) // 2))
                    sp.wait_ge(stored[1], 32 * (NT // 2))

                @block.vector
                def _(v):
                    pre = chain(v, v_step)
                    pre(v.tensor_tensor(z[:, :, :], acc_x[:, :, 0:H], own_n[:, :, :], ALU.add))
                    pre(v.reciprocal(z[:, :, :], z[:, :, :]))
                    v.wait_ge(bias_in, 16)
                    PER = 2 * H + 5

                    def back(n, slot, half):
                        step = chain(v, v_step, 2 + PER * n)
                        v.wait_ge(x_loaded[slot], 32 * (half + 1))
                        if not (type(n) is int and n < 2):
                            v.wait_ge(stored[slot], 32 * half)
                        nn = ds(n, 1)
                        for h in range(H):
                            cols = slice(h * C, (h + 1) * C)
                            step(v.scalar_tensor_tensor(val[:, slot:slot + 1, cols], xp_sb[:, slot:slot + 1, cols], own_n[:, nn, h],
                                                        acc[:, nn, cols], ALU.mult, ALU.add))
                        for h in range(H):
                            cols = slice(h * C, (h + 1) * C)
                            last = v.scalar_tensor_tensor(val[:, slot, cols], val[:, slot, cols], z[:, nn, h],
                                                          bias_sb[:, cols], ALU.mult, ALU.add)
                            if h < H - 1:
                                step(last)
                        last.then_inc(val_ready, 1)
                        v.wait_ge(relu_done, n + 1)
                        step(v.tensor_tensor(val[:, slot, :], val[:, slot, :], x_sb[:, slot, :], ALU.add))
                        v.sem_inc(x1_ready, 1)
                        if not (type(n) is int and n < 1):
                            v.wait_ge(h_ready, n)
                        for q in range(2):
                            step(v.bn_stats(stats[:, q, :], val[:, slot, q * HALF:(q + 1) * HALF]))
                        v.sem_inc(stats_ready, 1)
                        step(v.bn_aggr(mv[:, :], stats[:, :, :].rearrange("p a b -> p (a b)")))
                        step(v.tensor_scalar(mv[:, 1:2], mv[:, 1:2], EPS, None, ALU.add))
                        v.sem_inc(std_ready, 1)
                        v.wait_ge(norm_ready, 2 * n + 1)
                        step(v.reciprocal(rstd[:, :], rstd[:, :]))
                        v.tensor_scalar(shift[:, :], mv[:, 0:1], -1.0, rstd[:, 0:1], ALU.mult, ALU.mult).then_inc(norm_ready, 1)
                    each_tile(v, no_step, back)

                @block.scalar
                def _(a):
                    def back(n, slot, half):
                        a.wait_ge(val_ready, n + 1)
                        a.activation(val[:, slot, :], val[:, slot, :], ACT.Relu).then_inc(relu_done, 1)
                        a.wait_ge(std_ready, n + 1)
                        a.activation(rstd[:, :], mv[:, 1:2], ACT.Sqrt).then_inc(norm_ready, 1)
                        a.wait_ge(norm_ready, 2 * n + 2)
                        if not (type(n) is int and n < 2):
                            a.wait_ge(stored[slot], 32 * half)
                        a.activation(h_sb[:, slot, :], val[:, slot, :], ACT.Relu, bias=shift[:, 0:1],
                                     scale=rstd[:, 0:1]).then_inc(h_ready, 1)
                    each_tile(a, no_step, back)

        tables()
        with ExitStack() as gat:
            sb1, _, _ = opener(gat, "gat")
            att_n = sb1("att_n", [TN, NT, 2 * H])
            own_n = sb1("own_n", [TN, NT, H])
            top_n = sb1("top_n", [TN, NT, H])
            weight_e = sb1("weight_e", [P, NS, H + 1])
            project("proj", w_gat, x_in, xp_rows, norm=True, att=(att_src, att_dst))
            with ExitStack() as edge:
                att_e = opener(edge, "edge")[0]("att_e", [P, NS, H])
                attention_max()
                edge_weights()
            with ExitStack() as sums:
                sb2, _, _ = opener(sums, "sums")
                acc = sb2("acc", [TN, NT, D])
                acc_x = sb2("acc_x", [TN, NT, H + 1])
                aggregate("gagg", xp_rows, acc, acc_x)
                gat_finish(acc, acc_x)
        project("self0", w_self0, h_rows, part0_rows, bias=b0)
        with ExitStack() as sums:
            acc = opener(sums, "sum0")[0]("acc", [TN, NT, D])
            aggregate("agg0", h_rows, acc)
            project("neigh0", w_neigh0, None, h1_rows, acc=acc, add=part0_rows, relu=True)
        project("self1", w_self1, h1_rows, part1_rows, bias=b1, add=x1_rows)
        with ExitStack() as sums:
            acc = opener(sums, "sum1")[0]("acc", [TN, NT, D])
            aggregate("agg1", h1_rows, acc)
            project("neigh1", w_neigh1, None, out, acc=acc, add=part1_rows)


_INS = ['x', 'src', 'dst', 'L0_gnn_W', 'L0_gnn_att_src', 'L0_gnn_att_dst', 'L0_gnn_bias',
        'L1_gnn_W_self0', 'L1_gnn_W_neigh0', 'L1_gnn_b0', 'L1_gnn_W_self1', 'L1_gnn_W_neigh1', 'L1_gnn_b1']


def kernel(**inputs):
    import numpy as _np
    import concourse.bacc as _bacc
    from concourse import mybir as _mybir
    from concourse.bass_utils import run_bass_kernel_spmd as _run

    nc = _bacc.Bacc("TRN2", target_bir_lowering=False, num_devices=1)
    arrays, args = {}, []
    for name in _INS:
        a = _np.ascontiguousarray(inputs[name])
        arrays[f"in_{name}_dram"] = a
        args.append(nc.dram_tensor(f"in_{name}_dram", a.shape, _mybir.dt.from_np(a.dtype), kind="ExternalInput").ap())
    out = nc.dram_tensor("out_0_dram", inputs['x'].shape, _mybir.dt.float32, kind="ExternalOutput").ap()
    bass_gat_sage_sage(nc, *args, out)
    r = _run(nc, [arrays], core_ids=[0])
    return r.results[0]["out_0_dram"]
```

```python
import concourse.bass as bass
from concourse import mybir
from contextlib import ExitStack


def bass_gat_sage_sage(nc, x_in, src_in, dst_in, w_gat, att_src, att_dst, gat_bias,
                       w_self0, w_neigh0, b0, w_self1, w_neigh1, b1, out):
    f32, i32 = mybir.dt.float32, mybir.dt.int32
    f16, bf16 = mybir.dt.float16, mybir.dt.bfloat16
    ALU = mybir.AluOpType
    ACT = mybir.ActivationFunctionType
    X = mybir.AxisListType.X
    ds = bass.ds

    N, D = x_in.shape
    E = src_in.shape[0]
    H, C = att_src.shape
    P = 128
    TN = 125
    NT = N // TN
    CH = P
    CPP = 4
    EP = -(-E // (CPP * CH))
    NCH = EP * CPP
    NS = NCH + NT - 1
    SB = 4
    SP_ = NS // SB
    U = 4
    KT = D // P
    HALF = 512
    ROW = 2 * D + 2
    TOP = 14
    EXPONENT = 0x7F800000
    TINY = 1.0e-30
    FAR = 8192.0
    BIG = 1.0e30
    EPS = 1e-5
    SLOPE = 0.2
    assert NT * TN == N and NT % 2 == 1 and SP_ * SB == NS and NS % (2 * U) == 0 and H * C == D

    def tiles(ap):
        return ap.rearrange("(t p) d -> p t d", p=TN)

    def scratch(name, shape, dt=f32):
        return nc.dram_tensor(name, shape, dt).ap()

    edge_rows = scratch("edge_rows", (NCH, 2 * CH), i32)
    xp_rows = scratch("xp_rows", (N, D))
    att_rows = scratch("att_rows", (N, H))
    x1_rows = scratch("x1_rows", (N, D))
    h_rows = scratch("h_rows", (N, ROW), f16)
    part0_rows = scratch("part0_rows", (N, D))
    h1_rows = scratch("h1_rows", (N, ROW), f16)
    part1_rows = scratch("part1_rows", (N, D))
    weights = (w_gat, w_self0, w_neigh0, w_self1, w_neigh1)
    GAT, SELF0, NEIGH0, SELF1, NEIGH1 = range(5)
    split_w = [scratch(f"split_w{i}", (D, 2 * D), f16) for i in range(5)]

    def opener(ctx, tag):
        def sb(name, shape, dt=f32):
            return ctx.enter_context(nc.sbuf_tensor(f"{tag}_{name}", shape, dt))

        def ps(name, shape, dt=f32):
            return ctx.enter_context(nc.psum_tensor(f"{tag}_{name}", shape, dt))

        sems = []

        def sem(name):
            sems.append(nc.alloc_semaphore(f"{tag}_{name}"))
            return sems[-1]

        def clear():
            if sems:
                nc.clear_and_free_semaphores(sems)
                nc.all_engine_barrier()
        ctx.callback(clear)
        return sb, ps, sem

    def chain(eng, sem, start=0):
        done = [0]

        def step(ins):
            done[0] += 1
            ins.then_inc(sem, 1)
            eng.wait_ge(sem, start + done[0])
        step.done = done
        return step

    def scales(v, step, rows, largest, power, up, down):
        step(v.tensor_reduce(largest, rows, axis=X, op=ALU.max, apply_absolute_value=True))
        step(v.tensor_scalar(largest, largest, TINY, None, ALU.max))
        powers(v, step, largest, power, up, down)

    def powers(v, step, largest, power, up, down):
        step(v.tensor_scalar(power, largest.bitcast(i32), EXPONENT, None, ALU.bitwise_and))
        step(v.tensor_scalar(down, power.bitcast(f32), 2.0 ** -TOP, None, ALU.mult))
        step(v.tensor_scalar(up.bitcast(i32), power, -1.0, float((254 + TOP) << 23), ALU.mult, ALU.add))

    def each_tile(eng, ahead2, ahead1, last):
        ahead2(0, 0, 0)
        ahead2(1, 1, 0)
        ahead1(0, 0, 0)
        ahead1(1, 1, 0)
        ahead2(2, 0, 1)
        last(0, 0, 0)
        with eng.Fori(0, (NT - 3) // 2) as j:
            for u in range(2):
                ahead1(2 * j + (2 + u), u, j + 1)
                ahead2(2 * j + (3 + u), (1 + u) % 2, j + (3 + u) // 2)
                last(2 * j + (1 + u), (1 + u) % 2, j + (1 + u) // 2)
        ahead1(NT - 1, 0, (NT - 1) // 2)
        last(NT - 2, 1, (NT - 2) // 2)
        last(NT - 1, 0, (NT - 1) // 2)

    def nothing(*_):
        pass

    def early(n, k):
        return type(n) is int and n < k

    top = ExitStack()
    with top:
        sb0, _, _ = opener(top, "all")
        ident = sb0("ident", [P, P])
        iota_tn = sb0("iota_tn", [P, P])
        ident16 = sb0("ident16", [P, P], f16)
        w_down = sb0("w_down", [P, 6])
        w_att = sb0("w_att", [P, KT, 2 * H])
        w_att16 = sb0("w_att16", [P, KT, 2, 2 * H], f16)
        ones = sb0("ones", [P, P])
        idx = sb0("idx", [P, NS], i32)
        rel = sb0("rel", [P, NS])
        tile_of = sb0("tile_of", [1, NS], i32)
        deg_inv = sb0("deg_inv", [TN, NT])

        def tiles_of(engine, s, n):
            return nc.values_load_multi_w_load_instructions(
                tile_of[0:1, ds(s, n)], engines=[engine], min_val=0, max_val=NT - 1)[1]

        def tables():
            with ExitStack() as ctx:
                sb, ps, sem = opener(ctx, "tab")
                edges = sb("edges", [EP, CPP, 2, CH], i32)
                dst_f = sb("dst_f", [EP, CPP, CH])
                junk = sb("junk", [EP, CPP, CH])
                below = sb("below", [EP, NT - 1])
                start_i = sb("start_i", [P, NT - 1], i32)
                start_c = sb("start_c", [P, NT - 1])
                first = sb("first", [P, NT - 1])
                tile_no = sb("tile_no", [P, NT - 1])
                step_p = sb("step_p", [SP_, SB])
                step_r = sb("step_r", [1, NS])
                tile_r = sb("tile_r", [1, NS])
                junk2 = sb("junk2", [SP_, NT - 1])
                tile_p = sb("tile_p", [SP_, SB])
                lo_p = sb("lo_p", [SP_, SB])
                chunk_f = sb("chunk_f", [SP_, SB])
                chunk_i = sb("chunk_i", [SP_, SB], i32)
                got = sb("got", [SP_, SB, 2 * CH], i32)
                rel_p = sb("rel_p", [SP_, SB, CH])
                in_p = sb("in_p", [SP_, SB, CH])
                src_p = sb("src_p", [SP_, SB, CH])
                start_ps = ps("start_ps", [P, HALF])
                src_ps = ps("src_ps", [P, HALF])
                rel_ps = ps("rel_ps", [P, HALF])
                padded, loaded, stored = sem("padded"), sem("loaded"), sem("stored")
                made, counted, summed = sem("made"), sem("counted"), sem("summed")
                chunks_ready, rows_ready, turned = sem("chunks_ready"), sem("rows_ready"), sem("turned")
                fetched = [sem(f"fetched{b}") for b in range(SB)]
                v_step, g_step = sem("v_step"), sem("g_step")
                block = ctx.enter_context(nc.Block())
                whole = E // (CPP * CH)
                rest = E - whole * CPP * CH
                LOADS = 2 * (1 + -(-rest // CH))

                @block.sync
                def _(sp):
                    sp.wait_ge(padded, 1)
                    for k, ap in enumerate((src_in, dst_in)):
                        sp.dma_start(edges[0:whole, :, k, :],
                                     ap[0:whole * CPP * CH].rearrange("(p c e) -> p c e", c=CPP, e=CH)).then_inc(loaded, 16)
                        r = 0
                        for c in range(CPP):
                            n = min(CH, rest - r)
                            if n > 0:
                                sp.dma_start(edges[whole:whole + 1, c, k, 0:n],
                                             ap[whole * CPP * CH + r:whole * CPP * CH + r + n]
                                             .rearrange("(a n) -> a n", a=1)).then_inc(loaded, 16)
                                r += n
                    sp.wait_ge(loaded, LOADS * 16)
                    sp.dma_start(edge_rows.rearrange("(p c) e -> p (c e)", c=CPP),
                                 edges[:, :, :, :].rearrange("p c k e -> p (c k e)")).then_inc(stored, 16)
                    sp.wait_ge(stored, 16)

                @block.gpsimd
                def _(g):
                    step = chain(g, g_step)
                    g.iota(iota_tn[:, :], [[1, P]], base=0, channel_multiplier=0,
                           allow_small_or_imprecise_dtypes=True)
                    g.iota(tile_no[:, :], [[1, NT - 1]], base=1, channel_multiplier=0,
                           allow_small_or_imprecise_dtypes=True)
                    g.iota(step_p[:, :], [[SP_, SB]], base=0, channel_multiplier=1,
                           allow_small_or_imprecise_dtypes=True)
                    g.iota(step_r[:, :], [[1, NS]], base=0, channel_multiplier=0,
                           allow_small_or_imprecise_dtypes=True)
                    step(g.memset(ident[:, :], 0.0))
                    g.affine_select(out=ident[:, :], in_=ident[:, :], compare_op=ALU.not_equal, fill=1.0,
                                    base=0, pattern=[[-1, P]], channel_multiplier=1).then_inc(made, 1)
                    g.wait_ge(made, 1)
                    step(g.tensor_copy(ident16[:, :], ident[:, :]))
                    g.wait_ge(chunks_ready, 1)
                    g.wait_ge(stored, 16)
                    for b in range(SB):
                        g.indirect_dma_start(
                            out=got[:, b, :], out_offset=None, in_=edge_rows[:, :],
                            in_offset=bass.IndirectOffsetOnAxis(ap=chunk_i[:, b:b + 1], axis=0)).then_inc(fetched[b], 16)
                    for b in range(SB):
                        g.wait_ge(fetched[b], 16)

                @block.vector
                def _(v):
                    step = chain(v, v_step)
                    v.memset(edges[:, :, :, :], int(FAR)).then_inc(padded, 1)
                    step(v.memset(ones[:, :], 1.0))
                    v.wait_ge(loaded, LOADS * 16)
                    step(v.tensor_copy(dst_f[:, :, :], edges[:, :, 1, :]))
                    for t in range(1, NT):
                        last = v.tensor_scalar(junk[:, :, :], dst_f[:, :, :], float(t * TN), 0.0,
                                               ALU.is_lt, ALU.add, accum_out=below[:, t - 1:t])
                        if t < NT - 1:
                            step(last)
                    last.then_inc(counted, 1)
                    v.wait_ge(summed, 1)
                    step(v.tensor_copy(start_i[:, :], start_ps[:, 0:NT - 1]))
                    step(v.tensor_scalar(start_i[:, :], start_i[:, :], 7, None, ALU.arith_shift_right))
                    step(v.tensor_copy(start_c[:, :], start_i[:, :]))
                    v.wait_ge(made, 1)
                    step(v.tensor_tensor(first[:, :], start_c[:, :], tile_no[:, :], ALU.add))
                    for b in range(SB):
                        step(v.tensor_scalar(junk2[:, :], first[0:SP_, :], step_p[:, b:b + 1], 0.0,
                                             ALU.is_le, ALU.add, accum_out=tile_p[:, b:b + 1]))
                    step(v.tensor_tensor(chunk_f[:, :], step_p[:, :], tile_p[:, :], ALU.subtract))
                    step(v.tensor_scalar(lo_p[:, :], tile_p[:, :], float(TN), None, ALU.mult))
                    v.tensor_copy(chunk_i[:, :], chunk_f[:, :]).then_inc(chunks_ready, 1)
                    step(v.tensor_scalar(tile_r[:, :], step_r[:, :], first[0:1, 0:1], None, ALU.is_ge))
                    for t in range(1, NT - 1):
                        step(v.scalar_tensor_tensor(tile_r[:, :], step_r[:, :], first[0:1, t:t + 1],
                                                    tile_r[:, :], ALU.is_ge, ALU.add))
                    step(v.tensor_copy(tile_of[:, :], tile_r[:, :]))
                    for b in range(SB):
                        v.wait_ge(fetched[b], 16)
                        step(v.tensor_scalar(rel_p[:, b, :], got[:, b, CH:2 * CH], lo_p[:, b:b + 1], None,
                                             ALU.subtract))
                        step(v.tensor_scalar(in_p[:, b, :], rel_p[:, b, :], 0.0, None, ALU.is_ge))
                        step(v.scalar_tensor_tensor(in_p[:, b, :], rel_p[:, b, :], float(TN), in_p[:, b, :],
                                                    ALU.is_lt, ALU.mult))
                        step(v.tensor_scalar(in_p[:, b, :], in_p[:, b, :], -FAR, FAR, ALU.mult, ALU.add))
                        v.tensor_tensor(src_p[:, b, :], got[:, b, 0:CH], in_p[:, b, :], ALU.add).then_inc(rows_ready, 1)
                    v.wait_ge(turned, 1)
                    v.tensor_copy(idx[:, :], src_ps[:, 0:NS])
                    v.tensor_copy(rel[:, :], rel_ps[:, 0:NS])

                @block.tensor
                def _(t):
                    t.wait_ge(counted, 1)
                    t.matmul(start_ps[:, 0:NT - 1], ones[0:EP, :], below[:, :], start=True, stop=True).then_inc(summed, 1)
                    t.wait_ge(made, 1)
                    for b in range(SB):
                        t.wait_ge(rows_ready, b + 1)
                        t.transpose(src_ps[:, b * SP_:(b + 1) * SP_], src_p[:, b, :], ident[0:SP_, 0:SP_])
                        last = t.transpose(rel_ps[:, b * SP_:(b + 1) * SP_], rel_p[:, b, :], ident[0:SP_, 0:SP_])
                    last.then_inc(turned, 1)

        def split_weights():
            with ExitStack() as ctx:
                sb, ps, sem = opener(ctx, "wsp")
                w_sb = sb("w_sb", [P, 2, KT, D])
                w16 = sb("w16", [P, 2, KT, 2 * D], f16)
                att_sb = sb("att_sb", [P, 2, D])
                tmp = sb("tmp", [P, D])
                part_max = sb("part_max", [P, 6])
                all_max = sb("all_max", [P, 6])
                power = sb("power", [P, 6], i32)
                up = sb("up", [P, 6])
                loaded = [sem(f"loaded{i}") for i in range(2)]
                stored = [sem(f"stored{i}") for i in range(2)]
                att_loaded, v_step, max_ready, reduced = sem("att_loaded"), sem("v_step"), sem("max_ready"), sem("reduced")
                up_ready, hi_done, lo_done = sem("up_ready"), sem("hi_done"), sem("lo_done")
                block = ctx.enter_context(nc.Block())
                MATS = len(weights)

                @block.sync
                def _(sp):
                    for q, att in enumerate((att_src, att_dst)):
                        sp.dma_start(att_sb[:, q, :], att.rearrange("h c -> (h c)").partition_broadcast(P)).then_inc(att_loaded, 16)
                    for i in range(MATS):
                        if i >= 2:
                            sp.wait_ge(lo_done, i - 1)
                        sp.dma_start(w_sb[:, i % 2], weights[i].rearrange("(k p) n -> p k n", p=P)).then_inc(loaded[i % 2], 16)

                @block.gpsimd
                def _(g):
                    for i in range(MATS + 1):
                        g.wait_ge(max_ready, i + 1)
                        g.partition_all_reduce(all_max[:, i:i + 1], part_max[:, i:i + 1], P,
                                               bass.bass_isa.ReduceOp.max).then_inc(reduced, 1)
                        if i >= 1:
                            n = i - 1
                            g.wait_ge(lo_done, i)
                            g.dma_start(split_w[n].rearrange("(k p) n -> p k n", p=P), w16[:, n % 2]).then_inc(stored[n % 2], 16)
                    g.wait_ge(stored[0], 16 * ((MATS + 1) // 2))
                    g.wait_ge(stored[1], 16 * (MATS // 2))

                @block.scalar
                def _(a):
                    for i in range(MATS):
                        a.wait_ge(up_ready, i + 1)
                        if i >= 2:
                            a.wait_ge(stored[i % 2], 16 * (i // 2))
                        a.activation(w16[:, i % 2, :, 0:D], w_sb[:, i % 2], ACT.Copy, scale=up[:, i:i + 1]).then_inc(hi_done, 1)
                    a.wait_ge(up_ready, MATS + 1)
                    a.activation(w_att16[:, :, 0, :], w_att[:, :, :], ACT.Copy, scale=up[:, MATS:MATS + 1]).then_inc(hi_done, 1)

                @block.vector
                def _(v):
                    step = chain(v, v_step)

                    def largest(i, src):
                        step(v.tensor_reduce(part_max[:, i:i + 1], src, axis=X, op=ALU.max, apply_absolute_value=True))
                        v.tensor_scalar(part_max[:, i:i + 1], part_max[:, i:i + 1], TINY, None, ALU.max).then_inc(max_ready, 1)

                    def low(i, dst, src, hi):
                        v.wait_ge(reduced, i + 1)
                        c = slice(i, i + 1)
                        powers(v, step, all_max[:, c], power[:, c], up[:, c], w_down[:, c])
                        v.sem_inc(up_ready, 1)
                        v.wait_ge(hi_done, i + 1)
                        for k in range(KT):
                            last = v.scalar_tensor_tensor(dst(k), src(k), up[:, c], hi(k), ALU.mult, ALU.subtract)
                        last.then_inc(lo_done, 1)

                    def low_w(i):
                        low(i, lambda k: w16[:, i % 2, k, D:2 * D], lambda k: w_sb[:, i % 2, k, :],
                            lambda k: w16[:, i % 2, k, 0:D])

                    v.wait_ge(att_loaded, 32)
                    for i in range(MATS):
                        v.wait_ge(loaded[i % 2], 16 * (i // 2 + 1))
                        largest(i, w_sb[:, i % 2].rearrange("p k n -> p (k n)"))
                        if i == 0:
                            for k in range(KT):
                                for q in range(2):
                                    step(v.tensor_tensor(tmp[:, :], w_sb[:, 0, k, :], att_sb[:, q, :], ALU.mult))
                                    step(v.tensor_reduce(w_att[:, k, q * H:(q + 1) * H],
                                                         tmp[:, :].rearrange("p (h c) -> p h c", h=H), axis=X, op=ALU.add))
                        low_w(i)
                    largest(MATS, w_att[:, :, :].rearrange("p k n -> p (k n)"))
                    low(MATS, lambda k: w_att16[:, k, 1, :], lambda k: w_att[:, k, :], lambda k: w_att16[:, k, 0, :])

        def products(t, out_ps, a_t, w16, att=None):
            made = []
            for k in range(KT):
                for i, (pa, pw) in enumerate(((0, 0), (0, 1), (1, 0))):
                    for q in range(2):
                        made.append((out_ps[:, q * HALF:(q + 1) * HALF], a_t[:, pa, k, :],
                                     w16[:, k, pw * D + q * HALF:pw * D + (q + 1) * HALF]))
                    if att is not None:
                        made.append((att[:, 0:2 * H], a_t[:, pa, k, :], w_att16[:, k, pw, :]))
            per = len(made) // KT
            return [(o, l, r, n < per // 3, n >= len(made) - per // 3) for n, (o, l, r) in enumerate(made)]

        def project(tag, wi, rows_out, norm=None, acc=None, add=None, split=False):
            with ExitStack() as ctx:
                sb, ps, sem = opener(ctx, tag)
                w16 = sb("w16", [P, KT, 2 * D], f16)
                rows = sb("rows", [TN, 2, D])
                a16 = sb("a16", [P, 2, 2 * D], f16)
                a_t = [sb(f"a_t{i}", [P, 2, KT, P], f16) for i in range(2)]
                largest = sb("largest", [TN, 1])
                power = sb("power", [TN, 1], i32)
                up = sb("up", [TN, 1])
                down = sb("down", [TN, 1])
                post = sb("post", [TN, NT])
                if norm is not None:
                    x_sb = sb("x_sb", [TN, 2, D])
                    hn = sb("hn", [TN, D])
                    stats = sb("stats", [TN, 2, 6])
                    mv = sb("mv", [TN, 2])
                    rstd = sb("rstd", [TN, 1])
                    shift = sb("shift", [TN, 1])
                    post_att = sb("post_att", [TN, NT])
                    att_ps = ps("att_ps", [P, HALF])
                if split:
                    relu_sb = sb("relu_sb", [TN, D])
                    out16 = sb("out16", [TN, 2, ROW], f16)
                    outs = sb("out_up", [TN, 1]), sb("out_largest", [TN, 1]), sb("out_power", [TN, 1], i32)
                turn_ps = ps("turn_ps", [P, 2, KT, P], f16)
                out_ps = [ps(f"out_ps{i}", [P, D]) for i in range(2)]
                w_loaded, cleared = sem("w_loaded"), sem("cleared")
                x_loaded = [sem(f"x_loaded{i}") for i in range(2)]
                add_loaded = [sem(f"add_loaded{i}") for i in range(2)]
                stored = [sem(f"stored{i}") for i in range(2)]
                stats_ready, var_ready, std_ready, norm_ready = sem("stats_ready"), sem("var_ready"), sem("std_ready"), sem("norm_ready")
                hn_ready, up_ready, hi_done, lo_done = sem("hn_ready"), sem("up_ready"), sem("hi_done"), sem("lo_done")
                turned, hi_moved, lo_moved, mm_done = sem("turned"), sem("hi_moved"), sem("lo_moved"), sem("mm_done")
                read_out, out_ready, relu_done, out_up, out_hi = sem("read_out"), sem("out_ready"), sem("relu_done"), sem("out_up"), sem("out_hi")
                v_front, v_back, att_stored = sem("v_front"), sem("v_back"), sem("att_stored")
                block = ctx.enter_context(nc.Block())

                @block.sync
                def _(sp):
                    sp.dma_start(w16[:, :, :], split_w[wi].rearrange("(k p) n -> p k n", p=P)).then_inc(w_loaded, 16)

                    def front(m, slot, half):
                        if norm is not None:
                            if not early(m, 2):
                                sp.wait_ge(hn_ready, m - 1)
                            sp.dma_start(x_sb[:, slot:slot + 1, :], tiles(norm)[:, ds(m, 1), :]).then_inc(x_loaded[slot], 16)

                    def back(n, slot, half):
                        if add is not None:
                            if split:
                                if not early(n, 2):
                                    sp.wait_ge(out_ready, n - 1)
                            elif not early(n, 2):
                                sp.wait_ge(stored[slot], 16 * half)
                            sp.dma_start(rows[:, slot:slot + 1, :], tiles(add)[:, ds(n, 1), :]).then_inc(add_loaded[slot], 16)

                    each_tile(sp, front, nothing, back)

                @block.gpsimd
                def _(g):
                    def back(n, slot, half):
                        g.wait_ge(out_ready, n + 1)
                        src = out16 if split else rows
                        g.dma_start(tiles(rows_out)[:, ds(n, 1), :], src[:, slot:slot + 1, :]).then_inc(stored[slot], 16)
                    each_tile(g, nothing, nothing, back)
                    g.wait_ge(stored[0], 16 * ((NT + 1) // 2))
                    g.wait_ge(stored[1], 16 * (NT // 2))
                    if norm is not None:
                        g.dma_start(tiles(att_rows), att_n[:, :, 0:H]).then_inc(att_stored, 16)
                        g.wait_ge(att_stored, 16)

                @block.scalar
                def _(a):
                    def front(m, slot, half):
                        if norm is not None:
                            a.wait_ge(var_ready, m + 1)
                            a.activation(rstd[:, :], mv[:, 1:2], ACT.Sqrt).then_inc(std_ready, 1)
                            a.wait_ge(norm_ready, m + 1)
                            if not early(m, 1):
                                a.wait_ge(lo_done, m)
                            a.activation(hn[:, :], x_sb[:, slot, :], ACT.Relu, bias=shift[:, 0:1],
                                         scale=rstd[:, 0:1]).then_inc(hn_ready, 1)
                            src = hn[:, :]
                        else:
                            src = acc[:, ds(m, 1), :]
                        a.wait_ge(up_ready, m + 1)
                        if not early(m, 2):
                            a.wait_ge(turned, m - 1)
                        dst = a16[0:TN, slot, 0:D] if norm is not None else a16[0:TN, slot:slot + 1, 0:D]
                        a.wait_ge(cleared, 1)
                        a.activation(dst, src, ACT.Copy, scale=up[:, 0:1]).then_inc(hi_done, 1)

                    def turn(m, slot, half):
                        a.wait_ge(turned, m + 1)
                        if not early(m, 2):
                            a.wait_ge(mm_done, m - 1)
                        a.activation(a_t[slot][:, 0], turn_ps[:, 0], ACT.Copy).then_inc(hi_moved, 1)

                    def back(n, slot, half):
                        if split:
                            a.wait_ge(read_out, n + 1)
                            if not early(n, 1):
                                a.wait_ge(out_ready, n)
                            a.activation(relu_sb[:, :], rows[:, slot, :], ACT.Relu).then_inc(relu_done, 1)
                            a.wait_ge(out_up, n + 1)
                            if not early(n, 2):
                                a.wait_ge(stored[slot], 16 * half)
                            a.activation(out16[:, slot, 0:D], relu_sb[:, :], ACT.Copy, scale=up_o[:, 0:1]).then_inc(out_hi, 1)

                    up_o = outs[0] if split else None
                    each_tile(a, front, turn, back)

                @block.vector
                def _(v):
                    v.memset(a16[:, :, :], 0.0).then_inc(cleared, 1)
                    v.wait_ge(cleared, 1)
                    PF = (5 if norm is not None else 0) + 5 + 1
                    PB = 5 + 1 if split else 0

                    def front(m, slot, half):
                        step = chain(v, v_front, PF * m)
                        if norm is not None:
                            v.wait_ge(x_loaded[slot], 16 * (half + 1))
                            for q in range(2):
                                step(v.bn_stats(stats[:, q, :], x_sb[:, slot, q * HALF:(q + 1) * HALF]))
                            v.sem_inc(stats_ready, 1)
                            step(v.bn_aggr(mv[:, :], stats[:, :, :].rearrange("p a b -> p (a b)")))
                            v.tensor_scalar(mv[:, 1:2], mv[:, 1:2], EPS, None, ALU.add).then_inc(var_ready, 1)
                            v.wait_ge(std_ready, m + 1)
                            step(v.reciprocal(rstd[:, :], rstd[:, :]))
                            step(v.tensor_scalar(shift[:, :], mv[:, 0:1], -1.0, rstd[:, 0:1], ALU.mult, ALU.mult))
                            v.sem_inc(norm_ready, 1)
                            v.wait_ge(hn_ready, m + 1)
                            src = hn[:, :]
                        else:
                            src = acc[:, ds(m, 1), :]
                        scales(v, step, src, largest[:, :], power[:, :], up[:, :], down[:, :])
                        v.sem_inc(up_ready, 1)
                        m1 = ds(m, 1)
                        if norm is not None:
                            v.tensor_scalar(post_att[:, m1], down[:, :], w_down[0:TN, 5:6], None, ALU.mult)
                            step(v.tensor_scalar(post[:, m1], down[:, :], w_down[0:TN, wi:wi + 1], None, ALU.mult))
                        else:
                            step(v.tensor_scalar(post[:, m1], down[:, :], w_down[0:TN, wi:wi + 1],
                                                 deg_inv[:, m1], ALU.mult, ALU.mult))
                        v.wait_ge(hi_done, m + 1)
                        if norm is not None:
                            lo, hi = a16[0:TN, slot, D:2 * D], a16[0:TN, slot, 0:D]
                        else:
                            lo, hi = a16[0:TN, slot:slot + 1, D:2 * D], a16[0:TN, slot:slot + 1, 0:D]
                        v.scalar_tensor_tensor(lo, src, up[:, 0:1], hi, ALU.mult, ALU.subtract).then_inc(lo_done, 1)
                        assert step.done[0] == PF

                    def turn(m, slot, half):
                        v.wait_ge(turned, m + 1)
                        if not early(m, 2):
                            v.wait_ge(mm_done, m - 1)
                        v.tensor_copy(a_t[slot][:, 1], turn_ps[:, 1]).then_inc(lo_moved, 1)

                    def back(n, slot, half):
                        v.wait_ge(mm_done, n + 1)
                        if norm is not None:
                            v.tensor_scalar(att_n[:, ds(n, 1), :], att_ps[0:TN, 0:2 * H].rearrange("p (a k) -> p a k", a=1),
                                            post_att[:, ds(n, 1)], None, ALU.mult)
                        if add is not None:
                            v.wait_ge(add_loaded[slot], 16 * (half + 1))
                            last = v.scalar_tensor_tensor(rows[:, slot, :], out_ps[slot][0:TN, :], post[:, ds(n, 1)],
                                                          rows[:, slot, :], ALU.mult, ALU.add)
                        else:
                            if not early(n, 2):
                                v.wait_ge(stored[slot], 16 * half)
                            last = v.tensor_scalar(rows[:, slot, :], out_ps[slot][0:TN, :], post[:, ds(n, 1)], None, ALU.mult)
                        last.then_inc(read_out, 1)
                        if not split:
                            v.wait_ge(read_out, n + 1)
                            v.sem_inc(out_ready, 1)
                        else:
                            step = chain(v, v_back, PB * n)
                            v.wait_ge(relu_done, n + 1)
                            if not early(n, 2):
                                v.wait_ge(stored[slot], 16 * half)
                            scales(v, step, relu_sb[:, :], outs[1][:, :], outs[2][:, :], outs[0][:, :],
                                   out16[:, slot, 2 * D:ROW].bitcast(f32))
                            v.sem_inc(out_up, 1)
                            v.wait_ge(out_hi, n + 1)
                            step(v.scalar_tensor_tensor(out16[:, slot, D:2 * D], relu_sb[:, :], outs[0][:, 0:1],
                                                        out16[:, slot, 0:D], ALU.mult, ALU.subtract))
                            v.sem_inc(out_ready, 1)
                            assert step.done[0] == PB

                    each_tile(v, front, turn, back)

                @block.tensor
                def _(t):
                    def front(m, slot, half):
                        t.wait_ge(lo_done, m + 1)
                        if not early(m, 1):
                            t.wait_ge(hi_moved, m)
                            t.wait_ge(lo_moved, m)
                        for part in range(2):
                            for k in range(KT):
                                last = t.transpose(turn_ps[:, part, k, :], a16[:, slot, part * D + k * P:part * D + (k + 1) * P],
                                                   ident16[:, :])
                        last.then_inc(turned, 1)

                    def back(n, slot, half):
                        if early(n, 1):
                            t.wait_ge(w_loaded, 16)
                        t.wait_ge(hi_moved, n + 1)
                        t.wait_ge(lo_moved, n + 1)
                        if norm is not None and not early(n, 1):
                            t.wait_ge(read_out, n)
                        elif norm is None and not early(n, 2):
                            t.wait_ge(read_out, n - 1)
                        for o, l, r, start, stop in products(t, out_ps[slot], a_t[slot], w16, att_ps if norm is not None else None):
                            last = t.matmul(o, l, r, start=start, stop=stop)
                        last.then_inc(mm_done, 1)

                    each_tile(t, nothing, front, back)

        def attention_max():
            with ExitStack() as ctx:
                sb, ps, sem = opener(ctx, "max")
                idx_now = sb("idx_now", [P, 2, U], i32)
                fetched = sb("fetched", [P, 2, U, H])
                away = sb("away", [P, 2, U, TN])
                cand = sb("cand", [P, U, H, TN])
                top_s = sb("top_s", [TN, U, H])
                cand_ps = [ps(f"cand_ps{k}", [TN, H, P]) for k in range(U)]
                idx_ready, cleared = sem("idx_ready"), sem("cleared")
                arrived = [[sem(f"arrived{s}{k}") for k in range(U)] for s in range(2)]
                cand_ready, turned, v_step, used = sem("cand_ready"), sem("turned"), sem("v_step"), sem("used")
                reduced, issuing = sem("reduced"), sem("issuing")
                block = ctx.enter_context(nc.Block())

                @block.gpsimd
                def _(g):
                    last_row = g.to_reg(N - 1)
                    with g.Fori(0, NS // (2 * U)) as i:
                        for s in range(2):
                            g.wait_ge(used, 2 * i + (s + 1))
                            g.tensor_copy(idx_now[:, s, :], idx[:, ds(2 * U * i + U * s, U)]).then_inc(idx_ready, 1)
                            g.wait_ge(idx_ready, 2 * i + (s + 1))
                            g.sem_inc(issuing, 1)
                            for k in range(U):
                                g.indirect_dma_start(
                                    out=fetched[:, s, k, :], out_offset=None, in_=att_rows[:, :],
                                    in_offset=bass.IndirectOffsetOnAxis(ap=idx_now[:, s, k:k + 1], axis=0),
                                    bounds_check=last_row, oob_is_err=False).then_inc(arrived[s][k], 16)

                @block.vector
                def _(v):
                    first = chain(v, cleared)
                    first(v.memset(fetched[:, :, :, :], 0.0))
                    first(v.tensor_copy(top_n[:, :, :], att_n[:, :, 0:H]))
                    v.sem_inc(used, 2)
                    v.sem_inc(reduced, 1)
                    PER = 1 + 2 * U + U
                    with v.Fori(0, NS // (2 * U)) as i:
                        tile = tiles_of(mybir.EngineType.DVE, 2 * U * i, 2 * U)
                        for s in range(2):
                            step = chain(v, v_step, (2 * i + s) * (1 + U))
                            step(v.tensor_tensor(away[:, s], iota_tn[:, 0:TN].unsqueeze(1).to_broadcast([P, U, TN]),
                                                 rel[:, ds(2 * U * i + U * s, U)].unsqueeze(2).to_broadcast([P, U, TN]), ALU.not_equal))
                            v.wait_ge(turned, (2 * i + s) * U + 1)
                            for k in range(U):
                                v.wait_ge(arrived[s][k], 16 * (i + 1))
                                v.tensor_copy(att_e[:, ds(2 * U * i + (U * s + k), 1), :], fetched[:, s, k:k + 1, :])
                                last = v.scalar_tensor_tensor(
                                    cand[:, k], away[:, s, k:k + 1, :].to_broadcast([P, H, TN]), -BIG,
                                    fetched[:, s, k, :].unsqueeze(2).to_broadcast([P, H, TN]), ALU.mult, ALU.add)
                                last.then_inc(cand_ready, 1)
                            v.wait_ge(cand_ready, (2 * i + s + 1) * U)
                            v.sem_inc(used, 1)
                            for k in range(U):
                                v.wait_ge(turned, (2 * i + s) * U + (k + 2))
                                v.tensor_reduce(top_s[:, k, :], cand_ps[k][:, :, :], axis=X, op=ALU.max).then_inc(reduced, 1)
                            for k in range(U):
                                v.wait_ge(reduced, (2 * i + s) * U + (k + 2))
                                tl = ds(tile[U * s + k], 1)
                                step(v.tensor_tensor(top_n[:, tl, :], top_n[:, tl, :], top_s[:, k:k + 1, :], ALU.max))

                @block.tensor
                def _(t):
                    t.sem_inc(turned, 1)
                    with t.Fori(0, NS // U) as i:
                        for k in range(U):
                            t.wait_ge(cand_ready, U * i + (k + 1))
                            if k == 0:
                                t.wait_ge(reduced, U * i + 1)
                            for h in range(H):
                                last = t.transpose(cand_ps[k][:, h, :], cand[:, k, h, :], ident[:, :])
                            last.then_inc(turned, 1)

        def edge_weights():
            with ExitStack() as ctx:
                sb, ps, sem = opener(ctx, "wts")
                score_n = sb("score_n", [TN, NT, 2 * H])
                flat = sb("flat", [TN, NT, H])
                hot = sb("hot", [P, 2, U, TN])
                hot_t = sb("hot_t", [TN, 2, U, P])
                node_e = sb("node_e", [P, NS, 2 * H])
                raw = sb("raw", [P, NS, H])
                flat_e = sb("flat_e", [P, NS, H])
                hot_ps = [ps(f"hot_ps{i}", [TN, U, P]) for i in range(2)]
                node_ps = [ps(f"node_ps{i}", [P, U, 2 * H]) for i in range(2)]
                ready, hot_ready, turned, moved = sem("ready"), sem("hot_ready"), sem("turned"), sem("moved")
                spread, kept, v_step, raw_ready, own_ready = sem("spread"), sem("kept"), sem("v_step"), sem("raw_ready"), sem("own_ready")
                done = sem("done")
                block = ctx.enter_context(nc.Block())
                G = NS // U

                @block.vector
                def _(v):
                    step = chain(v, v_step)

                    def leaky(out_, in_, tmp_):
                        step(v.tensor_scalar(tmp_, in_, SLOPE, None, ALU.mult))
                        step(v.tensor_tensor(out_, in_, tmp_, ALU.max))
                    step(v.tensor_copy(score_n[:, :, H:2 * H], att_n[:, :, H:2 * H]))
                    step(v.tensor_tensor(top_n[:, :, :], top_n[:, :, :], att_n[:, :, H:2 * H], ALU.add))
                    leaky(score_n[:, :, 0:H], top_n[:, :, :], flat[:, :, :])
                    step(v.tensor_tensor(own_n[:, :, :], att_n[:, :, 0:H], att_n[:, :, H:2 * H], ALU.add))
                    leaky(own_n[:, :, :], own_n[:, :, :], flat[:, :, :])
                    step(v.tensor_tensor(own_n[:, :, :], own_n[:, :, :], score_n[:, :, 0:H], ALU.subtract))
                    v.sem_inc(ready, 1)
                    v.sem_inc(kept, 1)
                    with v.Fori(0, G // 2) as i:
                        for s in range(2):
                            v.wait_ge(kept, 2 * i + 1)
                            v.tensor_tensor(hot[:, s], iota_tn[:, 0:TN].unsqueeze(1).to_broadcast([P, U, TN]),
                                            rel[:, ds(2 * U * i + U * s, U)].unsqueeze(2).to_broadcast([P, U, TN]),
                                            ALU.is_equal).then_inc(hot_ready, 1)
                        for s in range(2):
                            v.wait_ge(spread, 2 * i + (s + 2))
                            v.tensor_copy(node_e[:, ds(2 * U * i + U * s, U), :], node_ps[s][:, :, :]).then_inc(kept, 1)
                    v.wait_ge(kept, G + 1)
                    step(v.tensor_tensor(raw[:, :, :], att_e[:, :, :], node_e[:, :, H:2 * H], ALU.add))
                    leaky(raw[:, :, :], raw[:, :, :], flat_e[:, :, :])
                    step(v.tensor_tensor(raw[:, :, :], raw[:, :, :], node_e[:, :, 0:H], ALU.subtract))
                    step(v.tensor_scalar(raw[:, :, :], raw[:, :, :], 0.0, None, ALU.min))
                    v.memset(weight_e[:, :, H:H + 1], 1.0)
                    v.sem_inc(raw_ready, 1)

                @block.scalar
                def _(a):
                    a.sem_inc(moved, 1)
                    with a.Fori(0, G // 2) as i:
                        for s in range(2):
                            a.wait_ge(turned, 2 * i + (s + 1))
                            a.wait_ge(spread, 2 * i + 1)
                            a.activation(hot_t[:, s], hot_ps[s][:, :, :], ACT.Copy).then_inc(moved, 1)
                    a.wait_ge(ready, 1)
                    a.activation(own_n[:, :, :], own_n[:, :, :], ACT.Exp)
                    a.wait_ge(raw_ready, 1)
                    a.activation(weight_e[:, :, 0:H], raw[:, :, :], ACT.Exp)

                @block.tensor
                def _(t):
                    t.wait_ge(ready, 1)
                    t.sem_inc(spread, 1)
                    with t.Fori(0, G // 2) as i:
                        tile = tiles_of(mybir.EngineType.PE, 2 * U * i, 2 * U)
                        for s in range(2):
                            t.wait_ge(hot_ready, 2 * i + (s + 1))
                            t.wait_ge(moved, 2 * i + 1)
                            for k in range(U):
                                last = t.transpose(hot_ps[s][:, k, :], hot[:, s, k, :], ident[:, :])
                            last.then_inc(turned, 1)
                        for s in range(2):
                            t.wait_ge(moved, 2 * i + (s + 2))
                            t.wait_ge(kept, 2 * i + 1)
                            for k in range(U):
                                last = t.matmul(node_ps[s][:, k, :], hot_t[:, s, k, :], score_n[:, ds(tile[U * s + k], 1), :],
                                                start=True, stop=True)
                            last.then_inc(spread, 1)

        def aggregate(tag, rows_in, acc, acc_x=None, product=None):
            with ExitStack() as ctx:
                sb, ps, sem = opener(ctx, tag)
                weighted = acc_x is not None
                R = 8
                B = 2 * R
                HOTS = 4
                rounds = NS // B
                assert rounds * B == NS and rounds == NT + 1
                idx_now = sb("idx_now", [P, 2, R], i32)
                if weighted:
                    got = sb("got", [P, R, D])
                    hot = sb("hot", [P, HOTS, P])
                    hot_w = sb("hot_w", [P, 2, H, P])
                    extra_ps = [ps(f"extra_ps{i}", [P, HALF]) for i in range(2)]
                else:
                    got = sb("got", [P, R, ROW], f16)
                    hot = sb("hot", [P, HOTS, P], bf16)
                if product is not None:
                    wi, bias, add, part = product
                    w16 = sb("w16", [P, KT, 2 * D], f16)
                    bias_sb = sb("bias_sb", [TN, D])
                    a16 = sb("a16", [P, ROW], f16)
                    a_t = sb("a_t", [P, 2, KT, P], f16)
                    rows = sb("rows", [TN, D])
                    post = sb("post", [TN, 1])
                    turn_ps = ps("turn_ps", [P, 2, KT, P], f16)
                    out_ps = ps("out_ps", [P, D])
                    w_loaded, x_loaded, add_loaded, stored = sem("w_loaded"), sem("x_loaded"), sem("add_loaded"), sem("stored")
                    turned, moved, prod_done = sem("turned"), sem("moved"), sem("prod_done")
                    post_ready, read_out, out_ready, cleared = sem("post_ready"), sem("read_out"), sem("out_ready"), sem("cleared")
                sum_ps = [ps(f"sum_ps{i}", [P, D]) for i in range(2)]
                idx_ready, hot_ready, hot_w_ready = sem("idx_ready"), sem("hot_ready"), sem("hot_w_ready")
                arrived = [sem(f"arrived{k}") for k in range(R)]
                issuing = sem("issuing")
                mm_done = sem("mm_done")
                added = sem("added")
                block = ctx.enter_context(nc.Block())

                @block.gpsimd
                def _(g):
                    last_row = g.to_reg(N - 1)
                    with g.Fori(0, rounds) as i:
                        for s in range(2):
                            g.wait_ge(mm_done, B * i + (R * s + 1))
                            g.tensor_copy(idx_now[:, s, :], idx[:, ds(B * i + R * s, R)]).then_inc(idx_ready, 1)
                            g.wait_ge(idx_ready, 2 * i + (s + 1))
                            g.sem_inc(issuing, 1)
                            for k in range(R):
                                g.wait_ge(mm_done, B * i + (R * s + k + 1))
                                g.sem_inc(issuing, 1)
                                g.indirect_dma_start(
                                    out=got[:, k, :], out_offset=None, in_=rows_in[:, :],
                                    in_offset=bass.IndirectOffsetOnAxis(ap=idx_now[:, s, k:k + 1], axis=0),
                                    bounds_check=last_row, oob_is_err=False).then_inc(arrived[k], 16)

                if product is not None:
                    @block.sync
                    def _(sp):
                        sp.dma_start(w16[:, :, :], split_w[wi].rearrange("(k p) n -> p k n", p=P)).then_inc(w_loaded, 16)
                        sp.dma_start(bias_sb[:, :], bias.partition_broadcast(TN)).then_inc(w_loaded, 16)
                        sp.wait_ge(cleared, 1)
                        sp.dma_start(a16[0:TN, :], rows_in[0:TN, :]).then_inc(x_loaded, 16)
                        sp.sem_inc(stored, 16)

                        def tile(i, ahead):
                            if add is not None:
                                sp.wait_ge(stored, 16 * i + 16)
                                sp.dma_start(rows[:, :], add[ds(i * TN, TN), :]).then_inc(add_loaded, 16)
                            if ahead:
                                sp.wait_ge(turned, i + 1)
                                sp.wait_ge(post_ready, i + 1)
                                sp.dma_start(a16[0:TN, :], rows_in[ds((i + 1) * TN, TN), :]).then_inc(x_loaded, 16)
                            sp.wait_ge(out_ready, i + 1)
                            sp.dma_start(part[ds(i * TN, TN), :], rows[:, :]).then_inc(stored, 16)

                        with sp.Fori(0, NT - 1) as i:
                            tile(i, True)
                        tile(NT - 1, False)
                        sp.wait_ge(stored, 16 * NT + 16)

                @block.vector
                def _(v):
                    v.memset(acc[:, :, :], 0.0)
                    if weighted:
                        v.memset(acc_x[:, :, :], 0.0)
                    if product is not None:
                        v.memset(a16[:, :], 0.0).then_inc(cleared, 1)
                    v.memset(got[:, :, :], 0.0)
                    v.drain()
                    v.sem_inc(mm_done, R)
                    v.sem_inc(added, 2)

                    def make_hot(i, u):
                        s = B * i + u
                        v.wait_ge(mm_done, s + (R - HOTS + 1))
                        if weighted:
                            v.tensor_scalar(hot[:, u % HOTS, :], iota_tn[:, :], rel[:, ds(s, 1)], None,
                                            ALU.is_equal).then_inc(hot_ready, 1)
                        else:
                            v.wait_ge(arrived[u % R], 16 * (2 * i + (u // R + 1)))
                            v.tensor_scalar(hot[:, u % HOTS, :], iota_tn[:, :], rel[:, ds(s, 1)],
                                            got[:, u % R, 2 * D:ROW].bitcast(f32), ALU.is_equal, ALU.mult).then_inc(hot_ready, 1)

                    def round_(i, prod):
                        tile = tiles_of(mybir.EngineType.DVE, B * i, B)
                        make_hot(i, 0)
                        make_hot(i, 1)
                        for u in range(B):
                            s = B * i + u
                            if u + 2 < B:
                                make_hot(i, u + 2)
                            v.wait_ge(mm_done, s + (R + 1))
                            v.wait_ge(added, s + 2)
                            tl = ds(tile[u], 1)
                            if weighted:
                                v.tensor_tensor(acc_x[:, tl, :], extra_ps[u % 2][0:TN, 0:H + 1].rearrange("p (a k) -> p a k", a=1),
                                                acc_x[:, tl, :], ALU.add)
                            v.tensor_tensor(acc[:, tl, :], sum_ps[u % 2][0:TN, :].rearrange("p (a d) -> p a d", a=1),
                                            acc[:, tl, :], ALU.add).then_inc(added, 1)
                            if prod and u == 1:
                                v.wait_ge(x_loaded, 16 * i + 16)
                                v.wait_ge(read_out, i + 1)
                                v.tensor_scalar(post[:, :], a16[0:TN, 2 * D:ROW].bitcast(f32), w_down[0:TN, wi:wi + 1], None,
                                                ALU.mult).then_inc(post_ready, 1)
                            if prod and u == B - 2:
                                v.wait_ge(prod_done, i + 2)
                                v.wait_ge(post_ready, i + 1)
                                if add is None:
                                    v.wait_ge(stored, 16 * i + 16)
                                    v.scalar_tensor_tensor(rows[:, :], out_ps[0:TN, :], post[:, 0:1], bias_sb[:, :],
                                                           ALU.mult, ALU.add).then_inc(read_out, 1)
                                    v.wait_ge(read_out, i + 2)
                                    v.sem_inc(out_ready, 1)
                                else:
                                    v.wait_ge(add_loaded, 16 * i + 16)
                                    v.scalar_tensor_tensor(rows[:, :], out_ps[0:TN, :], post[:, 0:1], rows[:, :],
                                                           ALU.mult, ALU.add).then_inc(read_out, 1)
                                    v.wait_ge(read_out, i + 2)
                                    v.tensor_tensor(rows[:, :], rows[:, :], bias_sb[:, :], ALU.add).then_inc(out_ready, 1)

                    if product is not None:
                        v.sem_inc(read_out, 1)
                        v.wait_ge(w_loaded, 32)
                        with v.Fori(0, rounds - 1) as i:
                            round_(i, True)
                        round_(rounds - 1, False)
                    else:
                        with v.Fori(0, rounds) as i:
                            round_(i, False)
                    if weighted:
                        v.wait_ge(added, NS + 2)
                        fin = chain(v, added, NS + 2)
                        fin(v.tensor_scalar(deg_inv[:, :], acc_x[:, :, H], 1.0, None, ALU.max))
                        fin(v.reciprocal(deg_inv[:, :], deg_inv[:, :]))

                if weighted:
                    @block.scalar
                    def _(a):
                        with a.Fori(0, rounds) as i:
                            for u in range(B):
                                s = B * i + u
                                a.wait_ge(hot_ready, s + 1)
                                a.wait_ge(mm_done, s + (R - 1))
                                for h in range(H):
                                    last = a.activation(hot_w[:, u % 2, h, :], hot[:, u % HOTS, :], ACT.Copy,
                                                        scale=weight_e[:, ds(s, 1), h])
                                last.then_inc(hot_w_ready, 1)
                elif product is not None:
                    @block.scalar
                    def _(a):
                        a.sem_inc(moved, 1)
                        with a.Fori(0, NT) as i:
                            a.wait_ge(turned, i + 1)
                            a.wait_ge(prod_done, i + 1)
                            for k in range(2):
                                last = a.activation(a_t[:, k], turn_ps[:, k], ACT.Copy)
                            last.then_inc(moved, 1)

                @block.tensor
                def _(t):
                    def round_(i, prod):
                        if prod:
                            todo = products(t, out_ps, a_t, w16)
                            first, per = 2, 4
                            t.wait_ge(x_loaded, 16 * i + 16)
                            t.wait_ge(moved, i + 1)
                            for part in range(2):
                                for k in range(KT):
                                    last = t.transpose(turn_ps[:, part, k, :], a16[:, part * D + k * P:part * D + (k + 1) * P],
                                                       ident16[:, :])
                            last.then_inc(turned, 1)
                        for u in range(B):
                            s = B * i + u
                            t.wait_ge(arrived[u % R], 16 * (2 * i + (u // R + 1)))
                            t.wait_ge(hot_w_ready if weighted else hot_ready, s + 1)
                            t.wait_ge(added, s + 1)
                            if weighted:
                                for h in range(H):
                                    t.matmul(sum_ps[u % 2][:, h * C:(h + 1) * C], hot_w[:, u % 2, h, :],
                                             got[:, u % R, h * C:(h + 1) * C], start=True, stop=True)
                                last = t.matmul(extra_ps[u % 2][:, 0:H + 1], hot[:, u % HOTS, :], weight_e[:, ds(s, 1), :],
                                                start=True, stop=True)
                            else:
                                for part in range(2):
                                    for q in range(2):
                                        cols = slice(part * D + q * HALF, part * D + (q + 1) * HALF)
                                        last = t.matmul(sum_ps[u % 2][:, q * HALF:(q + 1) * HALF], hot[:, u % HOTS, :],
                                                        got[:, u % R, cols], start=(part == 0), stop=(part == 1))
                            last.then_inc(mm_done, 1)
                            if prod and u == first:
                                t.wait_ge(moved, i + 2)
                                t.wait_ge(read_out, i + 1)
                            if prod and u >= first:
                                for o, l, r, start, stop in todo[(u - first) * per:(u - first + 1) * per]:
                                    last = t.matmul(o, l, r, start=start, stop=stop)
                                if (u - first + 1) * per == len(todo):
                                    last.then_inc(prod_done, 1)

                    if product is not None:
                        t.sem_inc(prod_done, 1)
                        t.wait_ge(w_loaded, 32)
                        with t.Fori(0, rounds - 1) as i:
                            round_(i, True)
                        round_(rounds - 1, False)
                    else:
                        with t.Fori(0, rounds) as i:
                            round_(i, False)

        def gat_finish(acc, acc_x):
            with ExitStack() as ctx:
                sb, ps, sem = opener(ctx, "fin")
                x_sb = sb("x_sb", [TN, 2, D])
                xp_sb = sb("xp_sb", [TN, 2, D])
                bias_sb = sb("bias_sb", [TN, D])
                val = sb("val", [TN, 2, D])
                h_sb = sb("h_sb", [TN, 2, D])
                h16 = sb("h16", [TN, 2, ROW], f16)
                z = sb("z", [TN, NT, H])
                stats = sb("stats", [TN, 2, 6])
                mv = sb("mv", [TN, 2, 2])
                rstd = sb("rstd", [TN, 2])
                shift = sb("shift", [TN, 2])
                largest = sb("largest", [TN, 1])
                power = sb("power", [TN, 1], i32)
                up = sb("up", [TN, 1])
                bias_in, stats_ready = sem("bias_in"), sem("stats_ready")
                x_loaded = [sem(f"x_loaded{i}") for i in range(2)]
                stored_x1 = [sem(f"stored_x1{i}") for i in range(2)]
                stored_h = [sem(f"stored_h{i}") for i in range(2)]
                v_pre, v_val, v_norm, v_split = sem("v_pre"), sem("v_val"), sem("v_norm"), sem("v_split")
                x1_ready, var_ready, std_ready, norm_ready = sem("x1_ready"), sem("var_ready"), sem("std_ready"), sem("norm_ready")
                h_ready, hi_done, up_ready, lo_done = sem("h_ready"), sem("hi_done"), sem("up_ready"), sem("lo_done")
                block = ctx.enter_context(nc.Block())

                @block.sync
                def _(sp):
                    sp.dma_start(bias_sb[:, :], gat_bias.partition_broadcast(TN)).then_inc(bias_in, 16)

                    def load(m, slot, half):
                        if not early(m, 2):
                            sp.wait_ge(x1_ready, m - 1)
                        sp.dma_start(x_sb[:, slot:slot + 1, :], tiles(x_in)[:, ds(m, 1), :]).then_inc(x_loaded[slot], 16)
                        sp.dma_start(xp_sb[:, slot:slot + 1, :], tiles(xp_rows)[:, ds(m, 1), :]).then_inc(x_loaded[slot], 16)

                    each_tile(sp, load, nothing, nothing)

                @block.gpsimd
                def _(g):
                    def store_x1(m, slot, half):
                        g.wait_ge(x1_ready, m + 1)
                        g.dma_start(tiles(x1_rows)[:, ds(m, 1), :], val[:, slot:slot + 1, :]).then_inc(stored_x1[slot], 16)

                    def store_h(n, slot, half):
                        g.wait_ge(lo_done, n + 1)
                        g.dma_start(tiles(h_rows)[:, ds(n, 1), :], h16[:, slot:slot + 1, :]).then_inc(stored_h[slot], 16)

                    each_tile(g, store_x1, nothing, store_h)
                    for stored in (stored_x1, stored_h):
                        g.wait_ge(stored[0], 16 * ((NT + 1) // 2))
                        g.wait_ge(stored[1], 16 * (NT // 2))

                @block.vector
                def _(v):
                    pre = chain(v, v_pre)
                    pre(v.tensor_tensor(z[:, :, :], acc_x[:, :, 0:H], own_n[:, :, :], ALU.add))
                    pre(v.reciprocal(z[:, :, :], z[:, :, :]))
                    v.wait_ge(bias_in, 16)

                    def values(m, slot, half):
                        PER = 2 + 1 + 3
                        step = chain(v, v_val, PER * m)
                        v.wait_ge(x_loaded[slot], 32 * (half + 1))
                        if not early(m, 2):
                            v.wait_ge(stored_x1[slot], 16 * half)
                            v.wait_ge(h_ready, m - 1)
                        mm = ds(m, 1)
                        for h in range(H):
                            cols = slice(h * C, (h + 1) * C)
                            last = v.scalar_tensor_tensor(val[:, slot:slot + 1, cols], xp_sb[:, slot:slot + 1, cols], own_n[:, mm, h],
                                                          acc[:, mm, cols], ALU.mult, ALU.add)
                        step(last)
                        for h in range(H):
                            cols = slice(h * C, (h + 1) * C)
                            last = v.scalar_tensor_tensor(val[:, slot, cols], val[:, slot, cols], z[:, mm, h],
                                                          bias_sb[:, cols], ALU.mult, ALU.add)
                        step(last)
                        step(v.scalar_tensor_tensor(val[:, slot, :], val[:, slot, :], 0.0, x_sb[:, slot, :], ALU.max, ALU.add))
                        v.sem_inc(x1_ready, 1)
                        for q in range(2):
                            last = v.bn_stats(stats[:, q, :], val[:, slot, q * HALF:(q + 1) * HALF])
                        step(last)
                        v.sem_inc(stats_ready, 1)
                        step(v.bn_aggr(mv[:, slot, :], stats[:, :, :].rearrange("p a b -> p (a b)")))
                        step(v.tensor_scalar(mv[:, slot, 1:2], mv[:, slot, 1:2], EPS, None, ALU.add))
                        v.sem_inc(var_ready, 1)
                        assert step.done[0] == PER

                    def normalize(m, slot, half):
                        step = chain(v, v_norm, 2 * m)
                        v.wait_ge(std_ready, m + 1)
                        step(v.reciprocal(rstd[:, slot:slot + 1], rstd[:, slot:slot + 1]))
                        step(v.tensor_scalar(shift[:, slot:slot + 1], mv[:, slot, 0:1], -1.0, rstd[:, slot:slot + 1],
                                             ALU.mult, ALU.mult))
                        v.sem_inc(norm_ready, 1)

                    def split(n, slot, half):
                        step = chain(v, v_split, 5 * n)
                        v.wait_ge(h_ready, n + 1)
                        if not early(n, 2):
                            v.wait_ge(stored_h[slot], 16 * half)
                        scales(v, step, h_sb[:, slot, :], largest[:, :], power[:, :], up[:, :],
                               h16[:, slot, 2 * D:ROW].bitcast(f32))
                        v.sem_inc(up_ready, 1)
                        v.wait_ge(hi_done, n + 1)
                        v.scalar_tensor_tensor(h16[:, slot, D:2 * D], h_sb[:, slot, :], up[:, 0:1], h16[:, slot, 0:D],
                                               ALU.mult, ALU.subtract).then_inc(lo_done, 1)
                    each_tile(v, values, normalize, split)

                @block.scalar
                def _(a):
                    def root(m, slot, half):
                        a.wait_ge(var_ready, m + 1)
                        a.activation(rstd[:, slot:slot + 1], mv[:, slot, 1:2], ACT.Sqrt).then_inc(std_ready, 1)

                    def normalize(m, slot, half):
                        a.wait_ge(norm_ready, m + 1)
                        if not early(m, 2):
                            a.wait_ge(lo_done, m - 1)
                        a.activation(h_sb[:, slot, :], val[:, slot, :], ACT.Relu, bias=shift[:, slot:slot + 1],
                                     scale=rstd[:, slot:slot + 1]).then_inc(h_ready, 1)

                    def split(n, slot, half):
                        a.wait_ge(up_ready, n + 1)
                        if not early(n, 2):
                            a.wait_ge(stored_h[slot], 16 * half)
                        a.activation(h16[:, slot, 0:D], h_sb[:, slot, :], ACT.Copy, scale=up[:, 0:1]).then_inc(hi_done, 1)
                    each_tile(a, root, normalize, split)

        tables()
        split_weights()
        with ExitStack() as gat:
            sb1, _, _ = opener(gat, "gat")
            att_n = sb1("att_n", [TN, NT, 2 * H])
            own_n = sb1("own_n", [TN, NT, H])
            top_n = sb1("top_n", [TN, NT, H])
            weight_e = sb1("weight_e", [P, NS, H + 1])
            project("proj", GAT, xp_rows, norm=x_in)
            with ExitStack() as edge:
                att_e = opener(edge, "edge")[0]("att_e", [P, NS, H])
                attention_max()
                edge_weights()
            with ExitStack() as sums:
                sb2, _, _ = opener(sums, "sums")
                acc = sb2("acc", [TN, NT, D])
                acc_x = sb2("acc_x", [TN, NT, H + 1])
                aggregate("gagg", xp_rows, acc, acc_x=acc_x)
                gat_finish(acc, acc_x)
        with ExitStack() as sums:
            acc = opener(sums, "sum0")[0]("acc", [TN, NT, D])
            aggregate("agg0", h_rows, acc, product=(SELF0, b0, None, part0_rows))
            project("neigh0", NEIGH0, h1_rows, acc=acc, add=part0_rows, split=True)
        with ExitStack() as sums:
            acc = opener(sums, "sum1")[0]("acc", [TN, NT, D])
            aggregate("agg1", h1_rows, acc, product=(SELF1, b1, x1_rows, part1_rows))
            project("neigh1", NEIGH1, out, acc=acc, add=part1_rows)


_INS = ['x', 'src', 'dst', 'L0_gnn_W', 'L0_gnn_att_src', 'L0_gnn_att_dst', 'L0_gnn_bias',
        'L1_gnn_W_self0', 'L1_gnn_W_neigh0', 'L1_gnn_b0', 'L1_gnn_W_self1', 'L1_gnn_W_neigh1', 'L1_gnn_b1']


def kernel(**inputs):
    import numpy as _np
    import concourse.bacc as _bacc
    from concourse import mybir as _mybir
    from concourse.bass_utils import run_bass_kernel_spmd as _run

    nc = _bacc.Bacc("TRN2", target_bir_lowering=False, num_devices=1)
    arrays, args = {}, []
    for name in _INS:
        a = _np.ascontiguousarray(inputs[name])
        arrays[f"in_{name}_dram"] = a
        args.append(nc.dram_tensor(f"in_{name}_dram", a.shape, _mybir.dt.from_np(a.dtype), kind="ExternalInput").ap())
    out = nc.dram_tensor("out_0_dram", inputs['x'].shape, _mybir.dt.float32, kind="ExternalOutput").ap()
    bass_gat_sage_sage(nc, *args, out)
    r = _run(nc, [arrays], core_ids=[0])
    return r.results[0]["out_0_dram"]
```

```python
import concourse.bass as bass
from concourse import mybir
from collections import namedtuple
from contextlib import ExitStack

Product = namedtuple("Product", "sync start scale finish move turn multiply row_moved prod_done w_loaded W_LOADS")


def bass_gat_sage_sage(nc, x_in, src_in, dst_in, w_gat, att_src, att_dst, gat_bias,
                       w_self0, w_neigh0, b0, w_self1, w_neigh1, b1, out):
    f32, i32 = mybir.dt.float32, mybir.dt.int32
    f16, bf16 = mybir.dt.float16, mybir.dt.bfloat16
    ALU = mybir.AluOpType
    ACT = mybir.ActivationFunctionType
    X = mybir.AxisListType.X
    ds = bass.ds

    N, D = x_in.shape
    E = src_in.shape[0]
    H, C = att_src.shape
    P = 128
    TN = 125
    NT = N // TN
    CH = P
    CPP = 4
    PAIR = 2
    RG = 8
    EP = -(-E // (CPP * CH))
    while (EP * CPP // PAIR + NT - 1) % RG:
        EP += 1
    NCH = EP * CPP
    NG = NCH // PAIR + NT - 1
    NS = PAIR * NG
    B = PAIR * RG
    ROUNDS = NG // RG
    SB = 4
    SP_ = NS // SB
    KT = D // P
    HALF = 512
    ROW = 2 * D + 2
    TOP = 14
    EXPONENT = 0x7F800000
    TINY = 1.0e-30
    FAR = 8192.0
    BIG = 1.0e30
    EPS = 1e-5
    UP = 2.0 ** (TOP + 1 - (D.bit_length() // 2))
    SLOPE = 0.2
    assert NT * TN == N and NT % 2 == 1 and SP_ * SB == NS and SP_ <= P and H * C == D and UP ** 2 * D <= 4.0 ** (TOP + 1) and ROUNDS > NT

    def tiles(ap):
        return ap.rearrange("(t p) d -> p t d", p=TN)

    def scratch(name, shape, dt=f32):
        return nc.dram_tensor(name, shape, dt).ap()

    edge_rows = scratch("edge_rows", (NCH, 2 * CH), i32)
    hn_rows = scratch("hn_rows", (N, ROW), f16)
    xp_rows = scratch("xp_rows", (N, D))
    xs_rows = scratch("xs_rows", (N, 2 * D), f16)
    att_rows = scratch("att_rows", (N, H))
    x1_rows = scratch("x1_rows", (N, D))
    h_rows = scratch("h_rows", (N, ROW), f16)
    part0_rows = scratch("part0_rows", (N, D))
    h1_rows = scratch("h1_rows", (N, ROW), f16)
    part1_rows = scratch("part1_rows", (N, D))
    weights = (w_gat, w_self0, w_neigh0, w_self1, w_neigh1)
    GAT, SELF0, NEIGH0, SELF1, NEIGH1 = range(5)
    split_w = [scratch(f"split_w{i}", (D, 2 * D), f16) for i in range(5)]

    def opener(ctx, tag):
        def sb(name, shape, dt=f32):
            return ctx.enter_context(nc.sbuf_tensor(f"{tag}_{name}", shape, dt))

        def ps(name, shape, dt=f32):
            return ctx.enter_context(nc.psum_tensor(f"{tag}_{name}", shape, dt))

        sems = []

        def sem(name):
            sems.append(nc.alloc_semaphore(f"{tag}_{name}"))
            return sems[-1]

        def clear():
            if sems:
                nc.clear_and_free_semaphores(sems)
                nc.all_engine_barrier()
        ctx.callback(clear)
        return sb, ps, sem

    def chain(eng, sem, start=0):
        done = [0]

        def step(ins):
            done[0] += 1
            ins.then_inc(sem, 1)
            eng.wait_ge(sem, start + done[0])
        step.done = done
        return step

    def scales(v, step, rows, largest, power, up, down):
        step(v.tensor_reduce(largest, rows, axis=X, op=ALU.max, apply_absolute_value=True))
        step(v.tensor_scalar(largest, largest, TINY, None, ALU.max))
        powers(v, step, largest, power, up, down)

    def powers(v, step, largest, power, up, down):
        step(v.tensor_scalar(power, largest.bitcast(i32), EXPONENT, None, ALU.bitwise_and))
        step(v.tensor_scalar(down, power.bitcast(f32), 2.0 ** -TOP, None, ALU.mult))
        step(v.tensor_scalar(up.bitcast(i32), power, -1.0, float((254 + TOP) << 23), ALU.mult, ALU.add))

    def each_tile(eng, ahead2, ahead1, last):
        ahead2(0, 0, 0)
        ahead2(1, 1, 0)
        ahead1(0, 0, 0)
        ahead1(1, 1, 0)
        ahead2(2, 0, 1)
        last(0, 0, 0)
        with eng.Fori(0, (NT - 3) // 2) as j:
            for u in range(2):
                ahead1(2 * j + (2 + u), u, j + 1)
                ahead2(2 * j + (3 + u), (1 + u) % 2, j + (3 + u) // 2)
                last(2 * j + (1 + u), (1 + u) % 2, j + (1 + u) // 2)
        ahead1(NT - 1, 0, (NT - 1) // 2)
        last(NT - 2, 1, (NT - 2) // 2)
        last(NT - 1, 0, (NT - 1) // 2)

    def nothing(*_):
        pass

    def both(first, second):
        def stage(*tile):
            first(*tile)
            second(*tile)
        return stage

    def early(n, k):
        return type(n) is int and n < k

    top = ExitStack()
    with top:
        sb0, _, _ = opener(top, "all")
        ident = sb0("ident", [P, P])
        iota_tn = sb0("iota_tn", [P, P])
        ident16 = sb0("ident16", [P, P], f16)
        ident_b = sb0("ident_b", [P, P], bf16)
        MATS = len(weights)
        EARLY = 4
        assert MATS == 5 and EARLY == 4
        w_up = sb0("w_up", [P, MATS + 1])
        w_down = sb0("w_down", [P, MATS + 1])
        w_att = sb0("w_att", [P, KT, 2 * H])
        w_att16 = sb0("w_att16", [P, KT, 2, 2 * H], f16)
        ones = sb0("ones", [P, P])
        idx = sb0("idx", [P, NS], i32)
        rel = sb0("rel", [P, NS])
        tile_of = sb0("tile_of", [1, NG], i32)
        deg_inv = sb0("deg_inv", [TN, NT])

        def tile_reg(engine, g):
            return nc.values_load_multi_w_load_instructions(
                tile_of[0:1, ds(g, 1)], engines=[engine], min_val=0, max_val=NT - 1)[1][0]

        def tables(key_r, mask_r):
            with ExitStack() as ctx:
                sb, ps, sem = opener(ctx, "tab")
                edges = sb("edges", [EP, CPP, 2, CH], i32)
                dst_f = sb("dst_f", [EP, CPP, CH])
                junk = sb("junk", [EP, CPP, CH])
                below = sb("below", [EP, NT - 1])
                start_i = sb("start_i", [P, NT - 1], i32)
                start_c = sb("start_c", [P, NT - 1])
                first = sb("first", [P, NT - 1])
                tile_no = sb("tile_no", [P, NT - 1])
                step_p = sb("step_p", [SP_, SB])
                group_p = sb("group_p", [SP_, SB])
                group_r = sb("group_r", [1, NG])
                tile_r = sb("tile_r", [1, NG])
                junk2 = sb("junk2", [SP_, NT - 1])
                tile_p = sb("tile_p", [SP_, SB])
                lo_p = sb("lo_p", [SP_, SB])
                chunk_f = sb("chunk_f", [SP_, SB])
                chunk_i = sb("chunk_i", [SP_, SB], i32)
                got = sb("got", [SP_, SB, 2 * CH], i32)
                rel_p = sb("rel_p", [SP_, SB, CH])
                in_p = sb("in_p", [SP_, SB, CH])
                src_p = sb("src_p", [SP_, SB, CH])
                start_ps = ps("start_ps", [P, HALF])
                src_ps = ps("src_ps", [P, HALF])
                rel_ps = ps("rel_ps", [P, HALF])
                padded, loaded, stored = sem("padded"), sem("loaded"), sem("stored")
                made, counted, summed = sem("made"), sem("counted"), sem("summed")
                chunks_ready, rows_ready, turned = sem("chunks_ready"), sem("rows_ready"), sem("turned")
                fetched = [sem(f"fetched{b}") for b in range(SB)]
                v_step, g_step = sem("v_step"), sem("g_step")
                block = ctx.enter_context(nc.Block())
                whole = E // (CPP * CH)
                rest = E - whole * CPP * CH
                LOADS = 2 * (1 + -(-rest // CH))

                @block.sync
                def _(sp):
                    sp.wait_ge(padded, 1)
                    for k, ap in enumerate((src_in, dst_in)):
                        sp.dma_start(edges[0:whole, :, k, :],
                                     ap[0:whole * CPP * CH].rearrange("(p c e) -> p c e", c=CPP, e=CH)).then_inc(loaded, 16)
                        r = 0
                        for c in range(CPP):
                            n = min(CH, rest - r)
                            if n > 0:
                                sp.dma_start(edges[whole:whole + 1, c, k, 0:n],
                                             ap[whole * CPP * CH + r:whole * CPP * CH + r + n]
                                             .rearrange("(a n) -> a n", a=1)).then_inc(loaded, 16)
                                r += n
                    sp.wait_ge(loaded, LOADS * 16)
                    sp.dma_start(edge_rows.rearrange("(p c) e -> p (c e)", c=CPP),
                                 edges[:, :, :, :].rearrange("p c k e -> p (c k e)")).then_inc(stored, 16)
                    sp.wait_ge(stored, 16)

                @block.gpsimd
                def _(g):
                    step = chain(g, g_step)
                    g.iota(iota_tn[:, :], [[1, P]], base=0, channel_multiplier=0,
                           allow_small_or_imprecise_dtypes=True)
                    g.iota(tile_no[:, :], [[1, NT - 1]], base=1, channel_multiplier=0,
                           allow_small_or_imprecise_dtypes=True)
                    g.iota(step_p[:, :], [[1, SB]], base=0, channel_multiplier=SB,
                           allow_small_or_imprecise_dtypes=True)
                    for half in range(SB // PAIR):
                        g.iota(group_p[:, half * PAIR:(half + 1) * PAIR], [[0, PAIR]], base=half,
                               channel_multiplier=SB // PAIR, allow_small_or_imprecise_dtypes=True)
                    g.iota(group_r[:, :], [[1, NG]], base=0, channel_multiplier=0,
                           allow_small_or_imprecise_dtypes=True)
                    step(g.memset(ident[:, :], 0.0))
                    g.affine_select(out=ident[:, :], in_=ident[:, :], compare_op=ALU.not_equal, fill=1.0,
                                    base=0, pattern=[[-1, P]], channel_multiplier=1).then_inc(made, 1)
                    g.wait_ge(made, 1)
                    step(g.tensor_copy(ident16[:, :], ident[:, :]))
                    step(g.tensor_copy(ident_b[:, :], ident[:, :]))
                    g.wait_ge(chunks_ready, 1)
                    g.wait_ge(stored, 16)
                    for b in range(SB):
                        g.indirect_dma_start(
                            out=got[:, b, :], out_offset=None, in_=edge_rows[:, :],
                            in_offset=bass.IndirectOffsetOnAxis(ap=chunk_i[:, b:b + 1], axis=0)).then_inc(fetched[b], 16)
                    for b in range(SB):
                        g.wait_ge(fetched[b], 16)

                @block.vector
                def _(v):
                    step = chain(v, v_step)
                    v.memset(edges[:, :, :, :], int(FAR)).then_inc(padded, 1)
                    step(v.memset(ones[:, :], 1.0))
                    v.wait_ge(loaded, LOADS * 16)
                    step(v.tensor_copy(dst_f[:, :, :], edges[:, :, 1, :]))
                    for t in range(1, NT):
                        last = v.tensor_scalar(junk[:, :, :], dst_f[:, :, :], float(t * TN), 0.0,
                                               ALU.is_lt, ALU.add, accum_out=below[:, t - 1:t])
                        if t < NT - 1:
                            step(last)
                    last.then_inc(counted, 1)
                    v.wait_ge(summed, 1)
                    step(v.tensor_copy(start_i[:, :], start_ps[:, 0:NT - 1]))
                    step(v.tensor_scalar(start_i[:, :], start_i[:, :], (PAIR * CH).bit_length() - 1, None, ALU.arith_shift_right))
                    step(v.tensor_copy(start_c[:, :], start_i[:, :]))
                    v.wait_ge(made, 1)
                    step(v.tensor_tensor(first[:, :], start_c[:, :], tile_no[:, :], ALU.add))
                    for b in range(SB):
                        step(v.tensor_scalar(junk2[:, :], first[0:SP_, :], group_p[:, b:b + 1], 0.0,
                                             ALU.is_le, ALU.add, accum_out=tile_p[:, b:b + 1]))
                    step(v.scalar_tensor_tensor(chunk_f[:, :], tile_p[:, :], -float(PAIR), step_p[:, :], ALU.mult, ALU.add))
                    step(v.tensor_scalar(lo_p[:, :], tile_p[:, :], float(TN), None, ALU.mult))
                    v.tensor_copy(chunk_i[:, :], chunk_f[:, :]).then_inc(chunks_ready, 1)
                    step(v.tensor_scalar(tile_r[:, :], group_r[:, :], first[0:1, 0:1], None, ALU.is_ge))
                    for t in range(1, NT - 1):
                        step(v.scalar_tensor_tensor(tile_r[:, :], group_r[:, :], first[0:1, t:t + 1],
                                                    tile_r[:, :], ALU.is_ge, ALU.add))
                    step(v.tensor_copy(tile_of[:, :], tile_r[:, :]))
                    for b in range(SB):
                        v.wait_ge(fetched[b], 16)
                        step(v.tensor_scalar(rel_p[:, b, :], got[:, b, CH:2 * CH], lo_p[:, b:b + 1], None,
                                             ALU.subtract))
                        step(v.tensor_scalar(in_p[:, b, :], rel_p[:, b, :], 0.0, None, ALU.is_ge))
                        step(v.scalar_tensor_tensor(in_p[:, b, :], rel_p[:, b, :], float(TN), in_p[:, b, :],
                                                    ALU.is_lt, ALU.mult))
                        step(v.tensor_scalar(in_p[:, b, :], in_p[:, b, :], -FAR, FAR, ALU.mult, ALU.add))
                        v.tensor_copy(key_r[:, b, :], got[:, b, CH:2 * CH])
                        v.tensor_scalar(mask_r[:, b, :], in_p[:, b, :], -BIG, None, ALU.mult)
                        v.tensor_tensor(src_p[:, b, :], got[:, b, 0:CH], in_p[:, b, :], ALU.add).then_inc(rows_ready, 1)
                    v.wait_ge(turned, 1)
                    for all_, ps_ in ((idx, src_ps), (rel, rel_ps)):
                        v.tensor_copy(all_[:, :].rearrange("p (s b) -> p s b", b=SB),
                                      ps_[:, 0:NS].rearrange("p (b s) -> p s b", b=SB))

                @block.tensor
                def _(t):
                    t.wait_ge(counted, 1)
                    t.matmul(start_ps[:, 0:NT - 1], ones[0:EP, :], below[:, :], start=True, stop=True).then_inc(summed, 1)
                    t.wait_ge(made, 1)
                    for b in range(SB):
                        t.wait_ge(rows_ready, b + 1)
                        t.transpose(src_ps[:, b * SP_:(b + 1) * SP_], src_p[:, b, :], ident[0:SP_, 0:SP_])
                        last = t.transpose(rel_ps[:, b * SP_:(b + 1) * SP_], rel_p[:, b, :], ident[0:SP_, 0:SP_])
                    last.then_inc(turned, 1)

        def weight_scales():
            with ExitStack() as ctx:
                sb, ps, sem = opener(ctx, "wsp")
                WS = 3
                w_sb = sb("w_sb", [P, WS, KT, D])
                w16 = sb("w16", [P, 2, KT, 2 * D], f16)
                att_sb = sb("att_sb", [P, 2, D])
                tmp = sb("tmp", [P, 2, D])
                part_max = sb("part_max", [P, MATS + 1])
                all_max = sb("all_max", [P, MATS + 1])
                power = sb("power", [P, MATS + 1], i32)
                loaded = [sem(f"loaded{i}") for i in range(WS)]
                tmp_ready, tmp_used = sem("tmp_ready"), sem("tmp_used")
                att_loaded, v_step, max_ready, reduced = sem("att_loaded"), sem("v_step"), sem("max_ready"), sem("reduced")
                up_ready, hi_done, lo_done = sem("up_ready"), sem("hi_done"), sem("lo_done")
                stored = [sem(f"stored{i}") for i in range(2)]
                block = ctx.enter_context(nc.Block())
                ORDER = [0, 1, MATS, *range(2, MATS)]
                SPLITS = [0, MATS, *range(1, EARLY)]

                @block.sync
                def _(sp):
                    def load(i):
                        sp.dma_start(w_sb[:, i % WS], weights[i].rearrange("(k p) n -> p k n", p=P)).then_inc(loaded[i % WS], 16)
                    load(0)
                    for q, att in enumerate((att_src, att_dst)):
                        sp.dma_start(att_sb[:, q, :], att.rearrange("h c -> (h c)").partition_broadcast(P)).then_inc(att_loaded, 16)
                    for i in range(1, WS):
                        load(i)
                    for i in range(EARLY):
                        sp.wait_ge(lo_done, SPLITS.index(i) + 1)
                        sp.dma_start(split_w[i].rearrange("(k p) n -> p k n", p=P), w16[:, i % 2]).then_inc(stored[i % 2], 16)
                        if i + WS < MATS:
                            load(i + WS)
                    for s in range(2):
                        sp.wait_ge(stored[s], 16 * ((EARLY + 1 - s) // 2))

                @block.gpsimd
                def _(g):
                    def reduce(i):
                        g.wait_ge(max_ready, ORDER.index(i) + 1)
                        g.partition_all_reduce(all_max[:, i:i + 1], part_max[:, i:i + 1], P,
                                               bass.bass_isa.ReduceOp.max).then_inc(reduced, 1)
                    g.wait_ge(att_loaded, 32)
                    g.wait_ge(loaded[0], 16)
                    for k in range(KT):
                        for q in range(2):
                            g.wait_ge(tmp_used, 2 * k + q + 1)
                            g.tensor_tensor(tmp[:, q, :], w_sb[:, 0, k, :], att_sb[:, q, :], ALU.mult).then_inc(tmp_ready, 1)
                    for i in ORDER:
                        reduce(i)

                @block.scalar
                def _(a):
                    for n, i in enumerate(SPLITS):
                        a.wait_ge(up_ready, n + 1)
                        if i < MATS and i >= 2:
                            a.wait_ge(stored[i % 2], 16 * (i // 2))
                        dst, of = (w_att16[:, :, 0, :], w_att[:, :, :]) if i == MATS else (w16[:, i % 2, :, 0:D], w_sb[:, i % WS])
                        a.activation(dst, of, ACT.Copy, scale=w_up[:, i:i + 1]).then_inc(hi_done, 1)

                @block.vector
                def _(v):
                    step = chain(v, v_step)

                    def largest(i, src):
                        step(v.tensor_reduce(part_max[:, i:i + 1], src, axis=X, op=ALU.max, apply_absolute_value=True))
                        v.tensor_scalar(part_max[:, i:i + 1], part_max[:, i:i + 1], TINY, None, ALU.max).then_inc(max_ready, 1)

                    def largest_w(i):
                        v.wait_ge(loaded[i % WS], 16 * (i // WS + 1))
                        largest(i, w_sb[:, i % WS].rearrange("p k n -> p (k n)"))

                    def scale(i):
                        v.wait_ge(reduced, ORDER.index(i) + 1)
                        c = slice(i, i + 1)
                        powers(v, step, all_max[:, c], power[:, c], w_up[:, c], w_down[:, c])

                    def low(c):
                        v.wait_ge(hi_done, SPLITS.index(c) + 1)
                        for k in range(KT):
                            if c == MATS:
                                dst, of, hi = w_att16[:, k, 1, :], w_att[:, k, :], w_att16[:, k, 0, :]
                            else:
                                dst, of, hi = w16[:, c % 2, k, D:2 * D], w_sb[:, c % WS, k, :], w16[:, c % 2, k, 0:D]
                            last = v.scalar_tensor_tensor(dst, of, w_up[:, c:c + 1], hi, ALU.mult, ALU.subtract)
                        last.then_inc(lo_done, 1)

                    v.sem_inc(tmp_used, 2)
                    largest_w(0)
                    for k in range(KT):
                        for q in range(2):
                            v.wait_ge(tmp_ready, 2 * k + q + 1)
                            v.tensor_reduce(w_att[:, k, q * H:(q + 1) * H], tmp[:, q, :].rearrange("p (h c) -> p h c", h=H),
                                            axis=X, op=ALU.add).then_inc(tmp_used, 1)
                        if k == KT // 2:
                            largest_w(1)
                    v.wait_ge(tmp_used, 2 * KT + 2)
                    largest(MATS, w_att[:, :, :].rearrange("p k n -> p (k n)"))
                    scale(0)
                    v.sem_inc(up_ready, 1)
                    largest_w(2)
                    for i in SPLITS[1:3]:
                        scale(i)
                        v.sem_inc(up_ready, 1)
                    low(0)
                    scale(2)
                    v.sem_inc(up_ready, 1)
                    low(MATS)
                    low(1)
                    largest_w(3)
                    low(2)
                    scale(3)
                    v.sem_inc(up_ready, 1)
                    largest_w(4)
                    low(3)
                    scale(4)

        def products(out_ps, a_t, w16):
            made = []
            for k in range(KT):
                for pa, pw in ((0, 0), (0, 1), (1, 0)):
                    for q in range(2):
                        made.append((out_ps[:, q * HALF:(q + 1) * HALF], a_t[:, pa, k, :],
                                     w16[:, k, pw * D + q * HALF:pw * D + (q + 1) * HALF]))
            return [(o, l, r, n < 2, n >= len(made) - 2) for n, (o, l, r) in enumerate(made)]

        def normalize_x():
            with ExitStack() as ctx:
                sb, ps, sem = opener(ctx, "norm")
                w_sb = sb("w_sb", [P, 2, KT, D])
                w16 = sb("w16", [P, KT, 2 * D], f16)
                w_loaded = [sem(f"w_loaded{i}") for i in range(2)]
                w_scaled, w_hi, w_lo, w_stored = sem("w_scaled"), sem("w_hi"), sem("w_lo"), sem("w_stored")
                x_sb = sb("x_sb", [TN, 2, D])
                hn = sb("hn", [TN, 2, D])
                a16 = sb("a16", [P, 2, ROW], f16)
                a_t = [sb(f"a_t{i}", [P, 2, KT, P], f16) for i in range(2)]
                stats = sb("stats", [TN, 2, 6])
                mv = sb("mv", [TN, 2, 2])
                rstd = sb("rstd", [TN, 2])
                shift = sb("shift", [TN, 2])
                post = sb("post", [TN, 1])
                turn_ps = [ps(f"turn_ps{i}", [P, 2, KT, P], f16) for i in range(2)]
                att_ps = ps("att_ps", [P, NT, 2 * H])
                x_loaded = [sem(f"x_loaded{i}") for i in range(2)]
                stored = [sem(f"stored{i}") for i in range(2)]
                cleared, var_ready, std_ready, norm_ready = sem("cleared"), sem("var_ready"), sem("std_ready"), sem("norm_ready")
                stats_ready, hn_ready, lo_done = sem("stats_ready"), sem("hn_ready"), sem("lo_done")
                turned, hi_moved, lo_moved, mm_done, read_out = sem("turned"), sem("hi_moved"), sem("lo_moved"), sem("mm_done"), sem("read_out")
                v_stats, v_norm, att_stored = sem("v_stats"), sem("v_norm"), sem("att_stored")
                block = ctx.enter_context(nc.Block())

                @block.sync
                def _(sp):
                    def load(m, slot, half):
                        if not early(m, 2):
                            sp.wait_ge(hn_ready, m - 1)
                        sp.dma_start(x_sb[:, slot:slot + 1, :], tiles(x_in)[:, ds(m, 1), :]).then_inc(x_loaded[slot], 16)

                    def store(n, slot, half):
                        sp.wait_ge(lo_done, n + 1)
                        sp.dma_start(tiles(hn_rows)[:, ds(n, 1), :], a16[0:TN, slot:slot + 1, :]).then_inc(stored[slot], 16)
                    each_tile(sp, load, nothing, store)
                    sp.wait_ge(stored[0], 16 * ((NT + 1) // 2))
                    sp.wait_ge(stored[1], 16 * (NT // 2))
                    sp.wait_ge(read_out, 1)
                    sp.dma_start(tiles(att_rows), att_n[:, :, 0:H]).then_inc(att_stored, 16)
                    sp.wait_ge(att_stored, 16)

                @block.gpsimd
                def _(g):
                    def load(i):
                        g.dma_start(w_sb[:, i % 2], weights[i].rearrange("(k p) n -> p k n", p=P)).then_inc(w_loaded[i % 2], 16)
                    load(EARLY)
                    for i in range(EARLY, MATS):
                        n = i - EARLY
                        if i + 1 < MATS:
                            load(i + 1)
                        g.wait_ge(w_loaded[i % 2], 16 * (n // 2 + 1))
                        if n > 0:
                            g.wait_ge(w_stored, 16 * n)
                        g.tensor_scalar(w_sb[:, i % 2], w_sb[:, i % 2], w_up[:, i:i + 1], None, ALU.mult).then_inc(w_scaled, 1)
                        g.wait_ge(w_scaled, n + 1)
                        g.tensor_copy(w16[:, :, 0:D], w_sb[:, i % 2]).then_inc(w_hi, 1)
                        g.wait_ge(w_hi, n + 1)
                        g.tensor_tensor(w16[:, :, D:2 * D], w_sb[:, i % 2], w16[:, :, 0:D], ALU.subtract).then_inc(w_lo, 1)
                        g.wait_ge(w_lo, n + 1)
                        g.dma_start(split_w[i].rearrange("(k p) n -> p k n", p=P), w16[:, :, :]).then_inc(w_stored, 16)
                    g.wait_ge(w_stored, 16 * (MATS - EARLY))

                @block.scalar
                def _(a):
                    a.wait_ge(cleared, 2)

                    def root(m, slot, half):
                        a.wait_ge(var_ready, m + 1)
                        a.activation(rstd[:, slot:slot + 1], mv[:, slot, 1:2], ACT.Sqrt).then_inc(std_ready, 1)

                    def normalize(m, slot, half):
                        a.wait_ge(norm_ready, m + 1)
                        if not early(m, 2):
                            a.wait_ge(lo_done, m - 1)
                            a.wait_ge(turned, m - 1)
                            a.wait_ge(stored[slot], 16 * half)
                        for dst in (hn[:, slot, :], a16[0:TN, slot, 0:D]):
                            last = a.activation(dst, x_sb[:, slot, :], ACT.Relu, bias=shift[:, slot:slot + 1],
                                                scale=rstd[:, slot:slot + 1])
                        last.then_inc(hn_ready, 1)

                    def move(n, slot, half):
                        if early(n, 1):
                            return
                        a.wait_ge(turned, n)
                        a.wait_ge(mm_done, n)
                        a.activation(a_t[1 - slot][:, 0], turn_ps[1 - slot][:, 0], ACT.Copy).then_inc(hi_moved, 1)
                    each_tile(a, nothing, both(root, normalize), move)
                    move(NT, NT % 2, NT // 2)

                @block.vector
                def _(v):
                    v.memset(a16[:, :, :], 0.0).then_inc(cleared, 1)
                    v.wait_ge(cleared, 1)
                    v.memset(a16[0:TN, :, 2 * D:ROW].bitcast(f32), 1.0 / UP)
                    v.tensor_scalar(post[:, :], w_down[0:TN, MATS:MATS + 1], 1.0 / UP, None, ALU.mult).then_inc(cleared, 1)
                    v.wait_ge(cleared, 2)

                    def statistics(m, slot, half):
                        step = chain(v, v_stats, 3 * m)
                        v.wait_ge(x_loaded[slot], 16 * (half + 1))
                        for q in range(2):
                            last = v.bn_stats(stats[:, q, :], x_sb[:, slot, q * HALF:(q + 1) * HALF])
                        step(last)
                        v.sem_inc(stats_ready, 1)
                        step(v.bn_aggr(mv[:, slot, :], stats[:, :, :].rearrange("p a b -> p (a b)")))
                        step(v.tensor_scalar(mv[:, slot, 1:2], mv[:, slot, 1:2], EPS, UP ** -2, ALU.add, ALU.mult))
                        v.sem_inc(var_ready, 1)

                    def normalize(m, slot, half):
                        step = chain(v, v_norm, 2 * m)
                        v.wait_ge(std_ready, m + 1)
                        step(v.reciprocal(rstd[:, slot:slot + 1], rstd[:, slot:slot + 1]))
                        step(v.tensor_scalar(shift[:, slot:slot + 1], mv[:, slot, 0:1], -1.0, rstd[:, slot:slot + 1],
                                             ALU.mult, ALU.mult))
                        v.sem_inc(norm_ready, 1)

                    def split(n, slot, half):
                        v.wait_ge(hn_ready, n + 1)
                        v.tensor_tensor(a16[0:TN, slot, D:2 * D], hn[:, slot, :], a16[0:TN, slot, 0:D],
                                        ALU.subtract).then_inc(lo_done, 1)
                        move(n, slot)

                    def move(n, slot):
                        if not early(n, 1):
                            v.wait_ge(turned, n)
                            v.wait_ge(mm_done, n)
                            v.tensor_copy(a_t[1 - slot][:, 1], turn_ps[1 - slot][:, 1]).then_inc(lo_moved, 1)
                    each_tile(v, nothing, both(statistics, normalize), split)
                    move(NT, NT % 2)
                    v.wait_ge(mm_done, NT + 2)
                    v.tensor_scalar(att_n[:, :, :], att_ps[0:TN, :, :], post[:, 0:1], None, ALU.mult).then_inc(read_out, 1)

                @block.tensor
                def _(t):
                    t.sem_inc(mm_done, 2)

                    def turn(n, slot, half):
                        t.wait_ge(lo_done, n + 1)
                        if not early(n, 2):
                            t.wait_ge(hi_moved, n - 1)
                            t.wait_ge(lo_moved, n - 1)
                        for part in range(2):
                            for k in range(KT):
                                last = t.transpose(turn_ps[slot][:, part, k, :], a16[:, slot, part * D + k * P:part * D + (k + 1) * P],
                                                   ident16[:, :])
                        last.then_inc(turned, 1)
                        multiply(n, 1 - slot)

                    def multiply(n, slot):
                        if early(n, 1):
                            return
                        t.wait_ge(hi_moved, n)
                        t.wait_ge(lo_moved, n)
                        todo = [(k, pa, pw) for k in range(KT) for pa, pw in ((0, 0), (0, 1), (1, 0))]
                        for i, (k, pa, pw) in enumerate(todo):
                            last = t.matmul(att_ps[:, ds(n - 1, 1), :], a_t[slot][:, pa, k, :], w_att16[:, k, pw, :],
                                            start=(i == 0), stop=(i == len(todo) - 1))
                        last.then_inc(mm_done, 1)
                    each_tile(t, nothing, nothing, turn)
                    multiply(NT, (NT - 1) % 2)

        def project(tag, wi, rows_out, acc, add, split=False, bounded=False):
            with ExitStack() as ctx:
                sb, ps, sem = opener(ctx, tag)
                w16 = sb("w16", [P, KT, 2 * D], f16)
                rows = sb("rows", [TN, 2, D])
                a16 = sb("a16", [P, 2, 2 * D], f16)
                a_t = [sb(f"a_t{i}", [P, 2, KT, P], f16) for i in range(2)]
                largest = sb("largest", [TN, 1])
                power = sb("power", [TN, 1], i32)
                up = sb("up", [TN, 1])
                down = sb("down", [TN, 1])
                mean_up = sb("mean_up", [TN, NT]) if bounded else None
                scales_ready = sem("scales_ready")
                post = sb("post", [TN, NT])
                if split:
                    relu_sb = sb("relu_sb", [TN, D])
                    out16 = sb("out16", [TN, 2, ROW], f16)
                    outs = sb("out_up", [TN, 1]), sb("out_largest", [TN, 1]), sb("out_power", [TN, 1], i32)
                turn_ps = ps("turn_ps", [P, 2, KT, P], f16)
                out_ps = [ps(f"out_ps{i}", [P, D]) for i in range(2)]
                w_loaded, cleared = sem("w_loaded"), sem("cleared")
                add_loaded = [sem(f"add_loaded{i}") for i in range(2)]
                stored = [sem(f"stored{i}") for i in range(2)]
                up_ready, hi_done, lo_done = sem("up_ready"), sem("hi_done"), sem("lo_done")
                turned, hi_moved, lo_moved, mm_done = sem("turned"), sem("hi_moved"), sem("lo_moved"), sem("mm_done")
                read_out, out_ready, relu_done, out_up, out_hi = sem("read_out"), sem("out_ready"), sem("relu_done"), sem("out_up"), sem("out_hi")
                v_front, v_back = sem("v_front"), sem("v_back")
                block = ctx.enter_context(nc.Block())

                @block.sync
                def _(sp):
                    sp.dma_start(w16[:, :, :], split_w[wi].rearrange("(k p) n -> p k n", p=P)).then_inc(w_loaded, 16)

                    def back(n, slot, half):
                        if not early(n, 2):
                            if split:
                                sp.wait_ge(out_ready, n - 1)
                            else:
                                sp.wait_ge(stored[slot], 16 * half)
                        sp.dma_start(rows[:, slot:slot + 1, :], tiles(add)[:, ds(n, 1), :]).then_inc(add_loaded[slot], 16)

                    each_tile(sp, back, nothing, nothing)

                @block.gpsimd
                def _(g):
                    def back(n, slot, half):
                        g.wait_ge(out_ready, n + 1)
                        src = out16 if split else rows
                        g.dma_start(tiles(rows_out)[:, ds(n, 1), :], src[:, slot:slot + 1, :]).then_inc(stored[slot], 16)
                    each_tile(g, nothing, nothing, back)
                    g.wait_ge(stored[0], 16 * ((NT + 1) // 2))
                    g.wait_ge(stored[1], 16 * (NT // 2))

                @block.scalar
                def _(a):
                    def front(m, slot, half):
                        src = acc[:, ds(m, 1), :]
                        if bounded:
                            a.wait_ge(scales_ready, 2)
                        else:
                            a.wait_ge(up_ready, m + 1)
                        if not early(m, 2):
                            a.wait_ge(turned, m - 1)
                        dst = a16[0:TN, slot:slot + 1, 0:D]
                        a.wait_ge(cleared, 1)
                        scale = mean_up[:, ds(m, 1)] if bounded else up[:, 0:1]
                        a.activation(dst, src, ACT.Copy, scale=scale).then_inc(hi_done, 1)

                    def turn(m, slot, half):
                        a.wait_ge(turned, m + 1)
                        if not early(m, 2):
                            a.wait_ge(mm_done, m - 1)
                        a.activation(a_t[slot][:, 0], turn_ps[:, 0], ACT.Copy).then_inc(hi_moved, 1)

                    def back(n, slot, half):
                        if split:
                            a.wait_ge(read_out, n + 1)
                            if not early(n, 1):
                                a.wait_ge(out_ready, n)
                            a.activation(relu_sb[:, :], rows[:, slot, :], ACT.Relu).then_inc(relu_done, 1)
                            a.wait_ge(out_up, n + 1)
                            if not early(n, 2):
                                a.wait_ge(stored[slot], 16 * half)
                            a.activation(out16[:, slot, 0:D], relu_sb[:, :], ACT.Copy, scale=up_o[:, 0:1]).then_inc(out_hi, 1)

                    up_o = outs[0] if split else None
                    each_tile(a, front, turn, back)

                @block.vector
                def _(v):
                    v.memset(a16[:, :, :], 0.0).then_inc(cleared, 1)
                    v.wait_ge(cleared, 1)
                    PF = 5 + 1
                    if bounded:
                        v.tensor_scalar(mean_up[:, :], deg_inv[:, :], UP, None, ALU.mult).then_inc(scales_ready, 1)
                        v.tensor_scalar(post[:, :], w_down[0:TN, wi:wi + 1].to_broadcast([TN, NT]), 1.0 / UP, None,
                                        ALU.mult).then_inc(scales_ready, 1)
                        v.wait_ge(scales_ready, 2)
                    PB = 5 + 1 if split else 0

                    def front(m, slot, half):
                        step = chain(v, v_front, PF * m)
                        src = acc[:, ds(m, 1), :]
                        m1 = ds(m, 1)
                        if not bounded:
                            scales(v, step, src, largest[:, :], power[:, :], up[:, :], down[:, :])
                            v.sem_inc(up_ready, 1)
                            step(v.tensor_scalar(post[:, m1], down[:, :], w_down[0:TN, wi:wi + 1],
                                                 deg_inv[:, m1], ALU.mult, ALU.mult))
                            assert step.done[0] == PF
                        v.wait_ge(hi_done, m + 1)
                        lo, hi = a16[0:TN, slot:slot + 1, D:2 * D], a16[0:TN, slot:slot + 1, 0:D]
                        scale = mean_up[:, m1] if bounded else up[:, 0:1]
                        v.scalar_tensor_tensor(lo, src, scale, hi, ALU.mult, ALU.subtract).then_inc(lo_done, 1)

                    def turn(m, slot, half):
                        v.wait_ge(turned, m + 1)
                        if not early(m, 2):
                            v.wait_ge(mm_done, m - 1)
                        v.tensor_copy(a_t[slot][:, 1], turn_ps[:, 1]).then_inc(lo_moved, 1)

                    def back(n, slot, half):
                        v.wait_ge(mm_done, n + 1)
                        v.wait_ge(add_loaded[slot], 16 * (half + 1))
                        v.scalar_tensor_tensor(rows[:, slot, :], out_ps[slot][0:TN, :], post[:, ds(n, 1)],
                                               rows[:, slot, :], ALU.mult, ALU.add).then_inc(read_out, 1)
                        if not split:
                            v.wait_ge(read_out, n + 1)
                            v.sem_inc(out_ready, 1)
                        else:
                            step = chain(v, v_back, PB * n)
                            v.wait_ge(relu_done, n + 1)
                            if not early(n, 2):
                                v.wait_ge(stored[slot], 16 * half)
                            scales(v, step, relu_sb[:, :], outs[1][:, :], outs[2][:, :], outs[0][:, :],
                                   out16[:, slot, 2 * D:ROW].bitcast(f32))
                            v.sem_inc(out_up, 1)
                            v.wait_ge(out_hi, n + 1)
                            step(v.scalar_tensor_tensor(out16[:, slot, D:2 * D], relu_sb[:, :], outs[0][:, 0:1],
                                                        out16[:, slot, 0:D], ALU.mult, ALU.subtract))
                            v.sem_inc(out_ready, 1)
                            assert step.done[0] == PB

                    each_tile(v, front, turn, back)

                @block.tensor
                def _(t):
                    def front(m, slot, half):
                        t.wait_ge(lo_done, m + 1)
                        if not early(m, 1):
                            t.wait_ge(hi_moved, m)
                            t.wait_ge(lo_moved, m)
                        for part in range(2):
                            for k in range(KT):
                                last = t.transpose(turn_ps[:, part, k, :], a16[:, slot, part * D + k * P:part * D + (k + 1) * P],
                                                   ident16[:, :])
                        last.then_inc(turned, 1)

                    def back(n, slot, half):
                        if early(n, 1):
                            t.wait_ge(w_loaded, 16)
                        t.wait_ge(hi_moved, n + 1)
                        t.wait_ge(lo_moved, n + 1)
                        if not early(n, 2):
                            t.wait_ge(read_out, n - 1)
                        for o, l, r, start, stop in products(out_ps[slot], a_t[slot], w16):
                            last = t.matmul(o, l, r, start=start, stop=stop)
                        last.then_inc(mm_done, 1)

                    each_tile(t, nothing, front, back)

        def product_beside(sb, ps, sem, wi, src_rows, part, bias=None, add=None, halves=None):
            w16 = sb("w16", [P, KT, 2 * D], f16)
            bias_sb = sb("bias_sb", [TN, D]) if bias is not None else None
            a16 = sb("a16", [P, ROW], f16)
            a_t = sb("a_t", [P, 2, KT, P], f16)
            rows = sb("rows", [TN, D])
            post = sb("post", [TN, 1])
            turn_ps = ps("turn_ps", [P, 2, KT, P], f16)
            out_ps = ps("out_ps", [P, D])
            w_loaded, x_loaded, stored = sem("w_loaded"), sem("x_loaded"), sem("stored")
            add_loaded = sem("add_loaded") if add is not None else None
            row_turned, row_moved, prod_done = sem("row_turned"), sem("row_moved"), sem("prod_done")
            post_ready, read_out, out_ready, cleared = sem("post_ready"), sem("read_out"), sem("out_ready"), sem("cleared")
            if halves is not None:
                parts16 = sb("parts16", [TN, 2 * D], f16)
                rows_ready, prod_hi = sem("rows_ready"), sem("prod_hi")
            STORES = 16 * (1 + (halves is not None))
            W_LOADS = 16 * (1 + (bias is not None))

            def sync(sp):
                sp.dma_start(w16[:, :, :], split_w[wi].rearrange("(k p) n -> p k n", p=P)).then_inc(w_loaded, 16)
                if bias is not None:
                    sp.dma_start(bias_sb[:, :], bias.partition_broadcast(TN)).then_inc(w_loaded, 16)
                sp.wait_ge(cleared, 1)
                sp.dma_start(a16[0:TN, :], src_rows[0:TN, :]).then_inc(x_loaded, 16)
                sp.sem_inc(stored, STORES)

                def tile(i, ahead):
                    if add is not None:
                        sp.wait_ge(stored, STORES * i + STORES)
                        sp.dma_start(rows[:, :], add[ds(i * TN, TN), :]).then_inc(add_loaded, 16)
                    if ahead:
                        sp.wait_ge(row_turned, i + 1)
                        sp.wait_ge(post_ready, i + 1)
                        sp.dma_start(a16[0:TN, :], src_rows[ds((i + 1) * TN, TN), :]).then_inc(x_loaded, 16)
                    sp.wait_ge(out_ready, i + 1)
                    sp.dma_start(part[ds(i * TN, TN), :], rows[:, :]).then_inc(stored, 16)
                    if halves is not None:
                        sp.dma_start(halves[ds(i * TN, TN), :], parts16[:, :]).then_inc(stored, 16)

                with sp.Fori(0, NT - 1) as i:
                    tile(i, True)
                tile(NT - 1, False)
                sp.wait_ge(stored, STORES * NT + STORES)

            def start(v):
                v.memset(a16[:, :], 0.0).then_inc(cleared, 1)
                v.sem_inc(read_out, 1)
                v.wait_ge(w_loaded, W_LOADS)

            def scale(v, i):
                v.wait_ge(x_loaded, 16 * i + 16)
                v.wait_ge(read_out, i + 1)
                v.tensor_scalar(post[:, :], a16[0:TN, 2 * D:ROW].bitcast(f32),
                                w_down[0:TN, wi:wi + 1] if halves is None else 1.0 / D, None,
                                ALU.mult).then_inc(post_ready, 1)

            def finish(v, i):
                v.wait_ge(prod_done, i + 2)
                v.wait_ge(post_ready, i + 1)
                if add is None:
                    v.wait_ge(stored, STORES * i + STORES)
                    if halves is not None:
                        v.tensor_scalar(rows[:, :], out_ps[0:TN, :], post[:, 0:1], None, ALU.mult).then_inc(rows_ready, 1)
                        v.wait_ge(rows_ready, i + 1)
                        v.sem_inc(read_out, 1)
                        v.tensor_copy(parts16[:, 0:D], rows[:, :]).then_inc(prod_hi, 1)
                        v.wait_ge(prod_hi, i + 1)
                        v.tensor_tensor(parts16[:, D:2 * D], rows[:, :], parts16[:, 0:D], ALU.subtract).then_inc(out_ready, 1)
                    else:
                        v.scalar_tensor_tensor(rows[:, :], out_ps[0:TN, :], post[:, 0:1], bias_sb[:, :],
                                               ALU.mult, ALU.add).then_inc(read_out, 1)
                        v.wait_ge(read_out, i + 2)
                        v.sem_inc(out_ready, 1)
                else:
                    v.wait_ge(add_loaded, 16 * i + 16)
                    v.scalar_tensor_tensor(rows[:, :], out_ps[0:TN, :], post[:, 0:1], rows[:, :],
                                           ALU.mult, ALU.add).then_inc(read_out, 1)
                    v.wait_ge(read_out, i + 2)
                    v.tensor_tensor(rows[:, :], rows[:, :], bias_sb[:, :], ALU.add).then_inc(out_ready, 1)

            def move(a, i):
                a.wait_ge(row_turned, i + 1)
                a.wait_ge(prod_done, i + 1)
                a.activation(a_t[:, :], turn_ps[:, :], ACT.Copy).then_inc(row_moved, 1)

            def turn(t, i):
                t.wait_ge(x_loaded, 16 * i + 16)
                t.wait_ge(row_moved, i + 1)
                for half in range(2):
                    for k in range(KT):
                        last = t.transpose(turn_ps[:, half, k, :], a16[:, half * D + k * P:half * D + (k + 1) * P], ident16[:, :])
                last.then_inc(row_turned, 1)

            def multiply(t, i, piece, pieces):
                todo = products(out_ps, a_t, w16)
                per = len(todo) // pieces
                assert per * pieces == len(todo)
                if piece == 0:
                    t.wait_ge(row_moved, i + 2)
                    t.wait_ge(read_out, i + 1)
                for o, l, r, first, final in todo[piece * per:(piece + 1) * per]:
                    last = t.matmul(o, l, r, start=first, stop=final)
                if piece == pieces - 1:
                    last.then_inc(prod_done, 1)

            return Product(sync, start, scale, finish, move, turn, multiply, row_moved, prod_done, w_loaded, W_LOADS)

        def edge_attention(pair_e, target_e):
            with ExitStack() as ctx:
                sb, ps, sem = opener(ctx, "edg")
                R = 8
                QU = 4
                idx_now = sb("idx_now", [P, 2, R], i32)
                fetched = sb("fetched", [P, 2, R, H])
                hot = sb("hot", [P, 4, QU, P], bf16)
                hot_t = sb("hot_t", [P, 2, QU, P])
                hot_ps = [ps(f"hot_ps{i}", [P, QU, P], bf16) for i in range(2)]
                node_ps = [ps(f"node_ps{i}", [P, QU, 2 * H]) for i in range(2)]
                prod = product_beside(sb, ps, sem, GAT, hn_rows, xp_rows, halves=xs_rows)
                att_now = sb("att_now", [TN, 2, QU // PAIR, 2 * H])
                idx_ready, issuing, used, cleared = sem("idx_ready"), sem("issuing"), sem("used"), sem("zeroed")
                arrived = [sem(f"arrived{s}") for s in range(2)]
                hot_ready = sem("hot_ready")
                hot_turned = sem("hot_turned")
                moved = sem("moved")
                spread = sem("spread")
                kept = sem("kept")
                block = ctx.enter_context(nc.Block())
                QUADS = B // QU
                assert QUADS == 4

                @block.sync
                def _(sp):
                    prod.sync(sp)

                @block.gpsimd
                def _(g):
                    last_row = g.to_reg(N - 1)
                    with g.Fori(0, ROUNDS) as i:
                        for s in range(2):
                            g.wait_ge(used, 2 * i + (s + 1))
                            g.tensor_copy(idx_now[:, s, :], idx[:, ds(B * i + R * s, R)]).then_inc(idx_ready, 1)
                            g.wait_ge(idx_ready, 2 * i + (s + 1))
                            g.sem_inc(issuing, 1)
                            for k in range(R):
                                g.indirect_dma_start(
                                    out=fetched[:, s, k, :], out_offset=None, in_=att_rows[:, :],
                                    in_offset=bass.IndirectOffsetOnAxis(ap=idx_now[:, s, k:k + 1], axis=0),
                                    bounds_check=last_row, oob_is_err=False).then_inc(arrived[s], 16)

                @block.vector
                def _(v):
                    v.memset(fetched[:, :, :, :], 0.0).then_inc(cleared, 1)
                    v.wait_ge(cleared, 1)
                    v.sem_inc(used, 2)
                    v.sem_inc(kept, 2)
                    prod.start(v)

                    def make_hot(i, q):
                        v.wait_ge(hot_turned, QUADS * i + (q + 1))
                        v.tensor_tensor(hot[:, q], iota_tn[:, :].unsqueeze(1).to_broadcast([P, QU, P]),
                                        rel[:, ds(B * i + QU * q, QU)].unsqueeze(2).to_broadcast([P, QU, P]),
                                        ALU.is_equal).then_inc(hot_ready, 1)

                    def keep(i, q):
                        v.wait_ge(spread, QUADS * i + (q + 3))
                        cols = ds(B * i + QU * q, QU)
                        v.tensor_copy(pair_e[:, cols, H:2 * H], node_ps[q % 2][:, :, 0:H])
                        v.tensor_copy(target_e[:, cols, :], node_ps[q % 2][:, :, H:2 * H]).then_inc(kept, 1)

                    def take(i, s):
                        v.wait_ge(arrived[s], 16 * R * (i + 1))
                        v.tensor_copy(pair_e[:, ds(B * i + R * s, R), 0:H], fetched[:, s]).then_inc(used, 1)

                    def round_(i, with_product, last=False):
                        for q in range(QUADS):
                            if q + 2 < QUADS:
                                make_hot(i, q + 2)
                            elif not last:
                                make_hot(i + 1, q + 2 - QUADS)
                            if with_product and q == 0:
                                prod.scale(v, i)
                            if q % 2 == 1:
                                take(i, q // 2)
                            keep(i, q)
                        if with_product:
                            prod.finish(v, i)

                    make_hot(0, 0)
                    make_hot(0, 1)
                    with v.Fori(0, NT) as i:
                        round_(i, True)
                    with v.Fori(NT, ROUNDS - 1) as i:
                        round_(i, False)
                    round_(ROUNDS - 1, False, last=True)

                @block.scalar
                def _(a):
                    a.sem_inc(moved, 2)
                    a.sem_inc(prod.row_moved, 1)

                    def round_(i, with_product):
                        for q in range(QUADS):
                            tile = [tile_reg(mybir.EngineType.Activation, RG * i + (QU // PAIR * q + n)) for n in range(QU // PAIR)]
                            a.wait_ge(spread, QUADS * i + (q + 1))
                            for n in range(QU // PAIR):
                                a.activation(att_now[:, q % 2, n:n + 1, :], att_n[:, ds(tile[n], 1), :], ACT.Copy)
                            a.wait_ge(hot_turned, QUADS * i + (q + 5))
                            a.activation(hot_t[:, q % 2], hot_ps[q % 2][:, :, :], ACT.Copy).then_inc(moved, 1)
                            if with_product and q == 0:
                                prod.move(a, i)
                    with a.Fori(0, NT) as i:
                        round_(i, True)
                    with a.Fori(NT, ROUNDS) as i:
                        round_(i, False)

                @block.tensor
                def _(t):
                    t.sem_inc(hot_turned, 4)
                    t.sem_inc(spread, 2)
                    t.sem_inc(prod.prod_done, 1)
                    t.wait_ge(prod.w_loaded, prod.W_LOADS)

                    def round_(i, with_product):
                        for q in range(QUADS):
                            t.wait_ge(hot_ready, QUADS * i + (q + 1))
                            t.wait_ge(moved, QUADS * i + (q + 1))
                            for k in range(QU):
                                last = t.transpose(hot_ps[q % 2][:, k, :], hot[:, q, k, :], ident_b[:, :])
                            last.then_inc(hot_turned, 1)
                            if with_product:
                                if q == 0:
                                    prod.turn(t, i)
                                else:
                                    prod.multiply(t, i, q - 1, QUADS - 1)
                            t.wait_ge(moved, QUADS * i + (q + 3))
                            t.wait_ge(kept, QUADS * i + (q + 1))
                            for k in range(QU):
                                last = t.matmul(node_ps[q % 2][:, k, :], hot_t[0:TN, q % 2, k, :],
                                                att_now[:, q % 2, k // PAIR, :], start=True, stop=True)
                            last.then_inc(spread, 1)
                    with t.Fori(0, NT) as i:
                        round_(i, True)
                    with t.Fori(NT, ROUNDS) as i:
                        round_(i, False)

        def edge_weights(pair_e, target_e, key_r, mask_r):
            with ExitStack() as ctx:
                sb, ps, sem = opener(ctx, "wts")
                ROWE = SB * CH
                cand_e = sb("cand_e", [P, NS, H])
                cand_r = sb("cand_r", [SP_, H, ROWE])
                fore = sb("fore", [SP_, H, ROWE])
                back = sb("back", [SP_, H, ROWE])
                anew = sb("anew", [SP_, ROWE + 1])
                ends = sb("ends", [SP_, 4, H])
                line = sb("line", [H, 4, SP_])
                link = sb("link", [H, SP_ + 1])
                whole = sb("whole", [H, SP_])
                through = sb("through", [H, SP_])
                carry = sb("carry", [H, 2, SP_])
                enter = sb("enter", [H, 2, SP_])
                enter_r = sb("enter_r", [SP_, 2, H])
                flat_e = sb("flat_e", [P, NS, H])
                row_ps = [ps(f"row_ps{h}", [P, HALF]) for h in range(H)]
                end_ps = [ps(f"end_ps{k}", [P, HALF]) for k in range(2)]
                cand_ready, turned, ends_ready, ends_turned = sem("cand_ready"), sem("turned"), sem("ends_ready"), sem("ends_turned")
                enter_ready, enter_turned, best_ready, best_turned = sem("enter_ready"), sem("enter_turned"), sem("best_ready"), sem("best_turned")
                v_step, raw_ready, exp_done, hi_ready = sem("v_step"), sem("raw_ready"), sem("exp_done"), sem("hi_ready")
                block = ctx.enter_context(nc.Block())

                @block.vector
                def _(v):
                    step = chain(v, v_step)
                    v.tensor_tensor(cand_e[:, :, :], pair_e[:, :, 0:H], pair_e[:, :, H:2 * H], ALU.max).then_inc(cand_ready, 1)
                    keys = key_r[:, :, :].rearrange("p b e -> p (b e)")
                    mask = mask_r[:, :, :].rearrange("p b e -> p (b e)")
                    v.memset(anew[:, 0:1], 0.0)
                    v.memset(anew[:, ROWE:ROWE + 1], 0.0)
                    step(v.tensor_tensor(anew[:, 1:ROWE], keys[:, 1:ROWE], keys[:, 0:ROWE - 1], ALU.not_equal))
                    step(v.tensor_scalar(anew[:, 1:ROWE], anew[:, 1:ROWE], -BIG, None, ALU.mult))
                    v.wait_ge(turned, 1)
                    for h in range(H):
                        last = v.tensor_tensor(cand_r[:, h, :], row_ps[h][0:SP_, :], mask, ALU.add)
                    step(last)

                    def scans(src, forward, dst):
                        for h in range(H):
                            if forward:
                                last = v.tensor_tensor_scan(dst[:, h, :], anew[:, 0:ROWE], src[:, h, :], -BIG, ALU.add, ALU.max)
                            else:
                                last = v.tensor_tensor_scan(dst[:, h, ::-1], anew[:, ROWE:0:-1], src[:, h, ::-1], -BIG, ALU.add, ALU.max)
                        return last
                    scans(cand_r, True, fore)
                    step(scans(cand_r, False, back))
                    v.tensor_copy(ends[:, 0, :], fore[:, :, ROWE - 1])
                    v.tensor_copy(ends[:, 1, :], back[:, :, 0])
                    v.tensor_copy(ends[:, 2, :], keys[:, 0:1].to_broadcast([SP_, H]))
                    v.tensor_copy(ends[:, 3, :], keys[:, ROWE - 1:ROWE].to_broadcast([SP_, H])).then_inc(ends_ready, 1)
                    v.wait_ge(ends_turned, 1)
                    step(v.tensor_copy(line[:, :, :], end_ps[0][0:H, 0:4 * SP_].rearrange("p (k s) -> p k s", k=4)))
                    v.memset(link[:, :], -BIG)
                    step(v.tensor_tensor(whole[:, :], line[:, 2, :], line[:, 3, :], ALU.not_equal))
                    step(v.tensor_tensor(link[:, 1:SP_], line[:, 2, 1:SP_], line[:, 3, 0:SP_ - 1], ALU.not_equal))
                    v.tensor_scalar(link[:, 1:SP_], link[:, 1:SP_], -BIG, None, ALU.mult)
                    step(v.tensor_scalar(whole[:, :], whole[:, :], -BIG, None, ALU.mult))
                    v.memset(enter[:, :, :], -BIG)
                    step(v.tensor_tensor(through[:, :], whole[:, :], link[:, 0:SP_], ALU.add))
                    step(v.tensor_tensor_scan(carry[:, 0, :], through[:, :], line[:, 0, :], -BIG, ALU.add, ALU.max))
                    step(v.tensor_tensor(through[:, :], whole[:, :], link[:, 1:SP_ + 1], ALU.add))
                    step(v.tensor_tensor_scan(carry[:, 1, ::-1], through[:, ::-1], line[:, 1, ::-1], -BIG, ALU.add, ALU.max))
                    v.tensor_tensor(enter[:, 0, 1:SP_], carry[:, 0, 0:SP_ - 1], link[:, 1:SP_], ALU.add)
                    v.tensor_tensor(enter[:, 1, 0:SP_ - 1], carry[:, 1, 1:SP_], link[:, 1:SP_], ALU.add).then_inc(enter_ready, 1)
                    v.wait_ge(enter_turned, 1)
                    step(v.tensor_copy(enter_r[:, :, :], end_ps[1][0:SP_, 0:2 * H].rearrange("p (k h) -> p k h", k=2)))
                    v.tensor_tensor(cand_r[:, :, 0], cand_r[:, :, 0], enter_r[:, 0, :], ALU.max)
                    step(v.tensor_tensor(cand_r[:, :, ROWE - 1], cand_r[:, :, ROWE - 1], enter_r[:, 1, :], ALU.max))
                    step(scans(cand_r, True, fore))
                    scans(fore, False, back).then_inc(best_ready, 1)
                    v.wait_ge(best_turned, 1)
                    for h in range(H):
                        last = v.tensor_tensor(cand_e[:, :, h].rearrange("p (s b) -> p s b", b=SB),
                                               row_ps[h][:, 0:NS].rearrange("p (b s) -> p s b", b=SB),
                                               target_e[:, :, h].rearrange("p (s b) -> p s b", b=SB), ALU.add)
                    step(last)
                    scored = [(cand_e[:, :, :], None), (pair_e[:, :, 0:H], target_e), (pair_e[:, :, H:2 * H], target_e)]
                    for at, more in scored:
                        if more is not None:
                            step(v.tensor_tensor(at, at, more[:, :, :], ALU.add))
                        step(v.tensor_scalar(flat_e[:, :, :], at, SLOPE, None, ALU.mult))
                        step(v.tensor_tensor(at, at, flat_e[:, :, :], ALU.max))
                    for q in range(2):
                        step(v.tensor_tensor(pair_e[:, :, q * H:(q + 1) * H], pair_e[:, :, q * H:(q + 1) * H], cand_e[:, :, :], ALU.subtract))
                    step(v.tensor_scalar(pair_e[:, :, :], pair_e[:, :, :], 0.0, None, ALU.min))
                    v.memset(weight_e[:, :, 0, 2 * H:2 * H + 1], 1.0)
                    v.memset(weight_e[:, :, 1, 2 * H:2 * H + 1], 0.0)
                    v.sem_inc(raw_ready, 1)
                    v.wait_ge(hi_ready, 1)
                    v.tensor_copy(high_e[:, :, :], weight_e[:, :, 0, 0:H])
                    v.scalar_tensor_tensor(weight_e[:, :, 1, 0:2 * H], pair_e[:, :, :], 2.0 ** TOP, weight_e[:, :, 0, 0:2 * H],
                                           ALU.mult, ALU.subtract)

                @block.scalar
                def _(a):
                    a.wait_ge(raw_ready, 1)
                    a.activation(pair_e[:, :, :], pair_e[:, :, :], ACT.Exp).then_inc(exp_done, 1)
                    a.wait_ge(exp_done, 1)
                    a.activation(weight_e[:, :, 0, 0:2 * H], pair_e[:, :, :], ACT.Copy, scale=2.0 ** TOP).then_inc(hi_ready, 1)

                @block.tensor
                def _(t):
                    t.wait_ge(cand_ready, 1)
                    for h in range(H):
                        for b in range(SB):
                            last = t.transpose(row_ps[h][0:SP_, b * CH:(b + 1) * CH], cand_e[:, :, h].rearrange("p (s b) -> p b s", b=SB)[:, b, :],
                                               ident[:, :])
                    last.then_inc(turned, 1)
                    t.wait_ge(ends_ready, 1)
                    for k in range(4):
                        last = t.transpose(end_ps[0][0:H, k * SP_:(k + 1) * SP_], ends[:, k, :], ident[0:SP_, 0:SP_])
                    last.then_inc(ends_turned, 1)
                    t.wait_ge(enter_ready, 1)
                    for k in range(2):
                        last = t.transpose(end_ps[1][0:SP_, k * H:(k + 1) * H], enter[:, k, :], ident[0:H, 0:H])
                    last.then_inc(enter_turned, 1)
                    t.wait_ge(best_ready, 1)
                    for h in range(H):
                        for b in range(SB):
                            last = t.transpose(row_ps[h][:, b * SP_:(b + 1) * SP_], back[:, h, b * CH:(b + 1) * CH],
                                               ident[0:SP_, 0:SP_])
                    last.then_inc(best_turned, 1)

        def aggregate(tag, rows_in, acc, acc_x=None, product=None):
            with ExitStack() as ctx:
                sb, ps, sem = opener(ctx, tag)
                weighted = acc_x is not None
                R = 8
                HOTS = R
                idx_now = sb("idx_now", [P, 2, R], i32)
                if weighted:
                    got = sb("got", [P, R, 2 * D], f16)
                    hot = sb("hot", [P, HOTS, P], f16)
                    hot_hi = sb("hot_hi", [P, HOTS, H, P], f16)
                    hot_lo = sb("hot_lo", [P, HOTS, H, P], f16)
                    extra_ps = [ps(f"extra_ps{i}", [P, HALF]) for i in range(2)]
                else:
                    got = sb("got", [P, R, ROW], f16)
                    hot = sb("hot", [P, HOTS, P], bf16)
                    wi, bias, add, part = product
                    prod = product_beside(sb, ps, sem, wi, rows_in, part, bias=bias, add=add)
                sum_ps = [ps(f"sum_ps{i}", [P, D]) for i in range(2)]
                idx_ready, hot_ready, hot_hi_ready, hot_lo_ready = sem("idx_ready"), sem("hot_ready"), sem("hot_hi_ready"), sem("hot_lo_ready")
                arrived = [sem(f"arrived{k}") for k in range(R)]
                issuing = sem("issuing")
                mm_done = sem("mm_done")
                added = sem("added")
                block = ctx.enter_context(nc.Block())

                @block.gpsimd
                def _(g):
                    last_row = g.to_reg(N - 1)
                    with g.Fori(0, ROUNDS) as i:
                        for s in range(B // R):
                            g.wait_ge(mm_done, B * i + (R * s + 1))
                            g.tensor_copy(idx_now[:, s, :], idx[:, ds(B * i + R * s, R)]).then_inc(idx_ready, 1)
                            g.wait_ge(idx_ready, 2 * i + (s + 1))
                            g.sem_inc(issuing, 1)
                            for k in range(R):
                                g.wait_ge(mm_done, B * i + (R * s + k + 1))
                                g.sem_inc(issuing, 1)
                                g.indirect_dma_start(
                                    out=got[:, k, :], out_offset=None, in_=rows_in[:, :],
                                    in_offset=bass.IndirectOffsetOnAxis(ap=idx_now[:, s, k:k + 1], axis=0),
                                    bounds_check=last_row, oob_is_err=False).then_inc(arrived[k], 16)

                if product is not None:
                    @block.sync
                    def _(sp):
                        prod.sync(sp)

                @block.vector
                def _(v):
                    v.memset(got[:, :, :].rearrange("p r d -> p (r d)").bitcast(f32), 0.0)
                    v.drain()
                    v.sem_inc(mm_done, R)
                    v.sem_inc(added, 2)
                    if product is not None:
                        prod.start(v)

                    def make_hots(i, n):
                        for u in range(PAIR * n, PAIR * (n + 1)):
                            s = B * i + u
                            v.wait_ge(mm_done, s + 1)
                            if weighted:
                                v.tensor_scalar(hot[:, u % HOTS, :], iota_tn[:, :], rel[:, ds(s, 1)], None,
                                                ALU.is_equal).then_inc(hot_ready, 1)
                            else:
                                v.wait_ge(arrived[u % R], 16 * (2 * i + (u // R + 1)))
                                v.tensor_scalar(hot[:, u % HOTS, :], iota_tn[:, :], rel[:, ds(s, 1)],
                                                got[:, u % R, 2 * D:ROW].bitcast(f32), ALU.is_equal, ALU.mult).then_inc(hot_ready, 1)
                        if weighted:
                            for u in range(PAIR * n, PAIR * (n + 1)):
                                s = B * i + u
                                v.wait_ge(hot_ready, s + 1)
                                v.tensor_tensor(hot_lo[:, u % HOTS, :, :], hot[:, u % HOTS:u % HOTS + 1, :].to_broadcast([P, H, P]),
                                                weight_e[:, ds(s, 1), 1, 0:H].rearrange("p a h -> p (a h)").unsqueeze(2).to_broadcast([P, H, P]),
                                                ALU.mult).then_inc(hot_lo_ready, 1)

                    AHEAD = 2 if weighted else 1

                    def round_(i, with_product, last=False):
                        tile = tile_reg(mybir.EngineType.DVE, RG * i)
                        for n in range(RG):
                            if n + AHEAD < RG:
                                make_hots(i, n + AHEAD)
                            elif not last:
                                make_hots(i + 1, n + AHEAD - RG)
                            if n + 1 < RG:
                                next_tile = tile_reg(mybir.EngineType.DVE, RG * i + (n + 1))
                            v.wait_ge(mm_done, B * i + (PAIR * (n + 1) + R))
                            v.wait_ge(added, RG * i + (n + 2))
                            tl = ds(tile, 1)
                            if weighted:
                                v.tensor_tensor(acc_x[:, tl, :], extra_ps[n % 2][0:TN, 0:2 * H + 1].rearrange("p (a k) -> p a k", a=1),
                                                acc_x[:, tl, :], ALU.add)
                            v.tensor_tensor(acc[:, tl, :], sum_ps[n % 2][0:TN, :].rearrange("p (a d) -> p a d", a=1),
                                            acc[:, tl, :], ALU.add).then_inc(added, 1)
                            tile = next_tile
                            if with_product and n == 0:
                                prod.scale(v, i)
                            if with_product and n == RG - 1:
                                prod.finish(v, i)

                    for n in range(AHEAD):
                        make_hots(0, n)
                    v.memset(acc[:, :, :], 0.0)
                    if weighted:
                        v.memset(acc_x[:, :, :], 0.0)
                    v.drain()
                    if product is not None:
                        with v.Fori(0, NT) as i:
                            round_(i, True)
                        with v.Fori(NT, ROUNDS - 1) as i:
                            round_(i, False)
                    else:
                        with v.Fori(0, ROUNDS - 1) as i:
                            round_(i, False)
                    round_(ROUNDS - 1, False, last=True)
                    if weighted:
                        v.wait_ge(added, NG + 2)
                        fin = chain(v, added, NG + 2)
                        fin(v.tensor_scalar(deg_inv[:, :], acc_x[:, :, 2 * H], 1.0, None, ALU.max))
                        fin(v.reciprocal(deg_inv[:, :], deg_inv[:, :]))

                @block.scalar
                def _(a):
                    if weighted:
                        with a.Fori(0, ROUNDS) as i:
                            for u in range(B):
                                s = B * i + u
                                a.wait_ge(hot_ready, s + 1)
                                a.wait_ge(mm_done, s + 1)
                                for h in range(H):
                                    last = a.activation(hot_hi[:, u % HOTS, h, :], hot[:, u % HOTS, :], ACT.Copy,
                                                        scale=high_e[:, ds(s, 1), h])
                                last.then_inc(hot_hi_ready, 1)
                    else:
                        a.sem_inc(prod.row_moved, 1)
                        with a.Fori(0, NT) as i:
                            prod.move(a, i)

                @block.tensor
                def _(t):
                    def round_(i, with_product):
                        if with_product:
                            prod.turn(t, i)
                        for n in range(RG):
                            t.wait_ge(added, RG * i + (n + 1))
                            steps = range(PAIR * n, PAIR * (n + 1))
                            if weighted:
                                for u in steps:
                                    t.wait_ge(arrived[u % R], 16 * (2 * i + (u // R + 1)))
                                t.wait_ge(hot_hi_ready, B * i + PAIR * (n + 1))
                                t.wait_ge(hot_lo_ready, B * i + PAIR * (n + 1))
                                for h in range(H):
                                    for u in steps:
                                        for k, (hot_k, part) in enumerate(((hot_hi, 0), (hot_hi, 1), (hot_lo, 0))):
                                            t.matmul(sum_ps[n % 2][:, h * C:(h + 1) * C], hot_k[:, u % HOTS, h, :],
                                                     got[:, u % R, part * D + h * C:part * D + (h + 1) * C],
                                                     start=(u == steps[0] and k == 0), stop=(u == steps[-1] and k == 2))
                                for u in steps:
                                    for part in range(2):
                                        last = t.matmul(extra_ps[n % 2][:, 0:2 * H + 1], hot[:, u % HOTS, :],
                                                        weight_e[:, ds(B * i + u, 1), part, :],
                                                        start=(u == steps[0] and part == 0), stop=(u == steps[-1] and part == 1))
                                    last.then_inc(mm_done, 1)
                            else:
                                for u in steps:
                                    t.wait_ge(arrived[u % R], 16 * (2 * i + (u // R + 1)))
                                    t.wait_ge(hot_ready, B * i + (u + 1))
                                    for part in range(2):
                                        for q in range(2):
                                            cols = slice(part * D + q * HALF, part * D + (q + 1) * HALF)
                                            last = t.matmul(sum_ps[n % 2][:, q * HALF:(q + 1) * HALF], hot[:, u % HOTS, :],
                                                            got[:, u % R, cols], start=(u == steps[0] and part == 0),
                                                            stop=(u == steps[-1] and part == 1))
                                    last.then_inc(mm_done, 1)
                            if with_product and 1 <= n < RG - 1:
                                prod.multiply(t, i, n - 1, RG - 2)

                    if product is not None:
                        t.sem_inc(prod.prod_done, 1)
                        t.wait_ge(prod.w_loaded, prod.W_LOADS)
                        with t.Fori(0, NT) as i:
                            round_(i, True)
                        with t.Fori(NT, ROUNDS) as i:
                            round_(i, False)
                    else:
                        with t.Fori(0, ROUNDS) as i:
                            round_(i, False)

        def gat_finish(acc, acc_x):
            with ExitStack() as ctx:
                sb, ps, sem = opener(ctx, "fin")
                x_sb = sb("x_sb", [TN, 2, D])
                xp_sb = sb("xp_sb", [TN, 2, D])
                bias_sb = sb("bias_sb", [TN, D])
                val = sb("val", [TN, 2, D])
                h_sb = sb("h_sb", [TN, 2, D])
                h16 = sb("h16", [TN, 2, ROW], f16)
                z = sb("z", [TN, NT, H])
                own_n = sb("own_n", [TN, NT, H])
                alone = sb("alone", [TN, NT])
                stats = sb("stats", [TN, 2, 6])
                mv = sb("mv", [TN, 2, 2])
                rstd = sb("rstd", [TN, 2])
                shift = sb("shift", [TN, 2])
                bias_in, stats_ready = sem("bias_in"), sem("stats_ready")
                x_loaded = [sem(f"x_loaded{i}") for i in range(2)]
                stored_x1 = [sem(f"stored_x1{i}") for i in range(2)]
                stored_h = [sem(f"stored_h{i}") for i in range(2)]
                v_pre, v_val, v_norm = sem("v_pre"), sem("v_val"), sem("v_norm")
                x1_ready, var_ready, std_ready, norm_ready = sem("x1_ready"), sem("var_ready"), sem("std_ready"), sem("norm_ready")
                h_ready, lo_done = sem("h_ready"), sem("lo_done")
                block = ctx.enter_context(nc.Block())

                @block.sync
                def _(sp):
                    sp.dma_start(bias_sb[:, :], gat_bias.partition_broadcast(TN)).then_inc(bias_in, 16)

                    def load(m, slot, half):
                        if not early(m, 2):
                            sp.wait_ge(x1_ready, m - 1)
                        sp.dma_start(x_sb[:, slot:slot + 1, :], tiles(x_in)[:, ds(m, 1), :]).then_inc(x_loaded[slot], 16)
                        sp.dma_start(xp_sb[:, slot:slot + 1, :], tiles(xp_rows)[:, ds(m, 1), :]).then_inc(x_loaded[slot], 16)

                    each_tile(sp, load, nothing, nothing)

                @block.gpsimd
                def _(g):
                    def store_x1(m, slot, half):
                        g.wait_ge(x1_ready, m + 1)
                        g.dma_start(tiles(x1_rows)[:, ds(m, 1), :], val[:, slot:slot + 1, :]).then_inc(stored_x1[slot], 16)

                    def store_h(n, slot, half):
                        g.wait_ge(lo_done, n + 1)
                        g.dma_start(tiles(h_rows)[:, ds(n, 1), :], h16[:, slot:slot + 1, :]).then_inc(stored_h[slot], 16)

                    each_tile(g, nothing, store_x1, store_h)
                    for stored in (stored_x1, stored_h):
                        g.wait_ge(stored[0], 16 * ((NT + 1) // 2))
                        g.wait_ge(stored[1], 16 * (NT // 2))

                @block.vector
                def _(v):
                    pre = chain(v, v_pre)
                    pre(v.tensor_scalar(alone[:, :], acc_x[:, :, 2 * H], 0.5, 2.0 ** TOP, ALU.is_lt, ALU.mult))
                    pre(v.tensor_tensor(own_n[:, :, :], acc_x[:, :, H:2 * H], deg_inv[:, :].unsqueeze(2).to_broadcast([TN, NT, H]), ALU.mult))
                    pre(v.tensor_tensor(own_n[:, :, :], own_n[:, :, :], alone[:, :].unsqueeze(2).to_broadcast([TN, NT, H]), ALU.add))
                    pre(v.tensor_tensor(z[:, :, :], acc_x[:, :, 0:H], own_n[:, :, :], ALU.add))
                    pre(v.reciprocal(z[:, :, :], z[:, :, :]))
                    pre(v.tensor_scalar(z[:, :, :], z[:, :, :], w_down[0:TN, GAT:GAT + 1], float(D), ALU.mult, ALU.mult))
                    pre(v.memset(h16[:, :, 2 * D:ROW].bitcast(f32), 1.0 / UP))
                    v.wait_ge(bias_in, 16)

                    def values(m, slot, half):
                        PER = 2 + 1 + 3
                        step = chain(v, v_val, PER * m)
                        v.wait_ge(x_loaded[slot], 32 * (half + 1))
                        if not early(m, 2):
                            v.wait_ge(stored_x1[slot], 16 * half)
                            v.wait_ge(h_ready, m - 1)
                        mm = ds(m, 1)
                        for h in range(H):
                            cols = slice(h * C, (h + 1) * C)
                            last = v.scalar_tensor_tensor(val[:, slot:slot + 1, cols], xp_sb[:, slot:slot + 1, cols], own_n[:, mm, h],
                                                          acc[:, mm, cols], ALU.mult, ALU.add)
                        step(last)
                        for h in range(H):
                            cols = slice(h * C, (h + 1) * C)
                            last = v.scalar_tensor_tensor(val[:, slot, cols], val[:, slot, cols], z[:, mm, h],
                                                          bias_sb[:, cols], ALU.mult, ALU.add)
                        step(last)
                        step(v.scalar_tensor_tensor(val[:, slot, :], val[:, slot, :], 0.0, x_sb[:, slot, :], ALU.max, ALU.add))
                        v.sem_inc(x1_ready, 1)
                        for q in range(2):
                            last = v.bn_stats(stats[:, q, :], val[:, slot, q * HALF:(q + 1) * HALF])
                        step(last)
                        v.sem_inc(stats_ready, 1)
                        step(v.bn_aggr(mv[:, slot, :], stats[:, :, :].rearrange("p a b -> p (a b)")))
                        step(v.tensor_scalar(mv[:, slot, 1:2], mv[:, slot, 1:2], EPS, UP ** -2, ALU.add, ALU.mult))
                        v.sem_inc(var_ready, 1)
                        assert step.done[0] == PER

                    def normalize(m, slot, half):
                        step = chain(v, v_norm, 2 * m)
                        v.wait_ge(std_ready, m + 1)
                        step(v.reciprocal(rstd[:, slot:slot + 1], rstd[:, slot:slot + 1]))
                        step(v.tensor_scalar(shift[:, slot:slot + 1], mv[:, slot, 0:1], -1.0, rstd[:, slot:slot + 1],
                                             ALU.mult, ALU.mult))
                        v.sem_inc(norm_ready, 1)

                    def split(n, slot, half):
                        v.wait_ge(h_ready, n + 1)
                        v.tensor_tensor(h16[:, slot, D:2 * D], h_sb[:, slot, :], h16[:, slot, 0:D], ALU.subtract).then_inc(lo_done, 1)
                    each_tile(v, nothing, both(values, normalize), split)

                @block.scalar
                def _(a):
                    def root(m, slot, half):
                        a.wait_ge(var_ready, m + 1)
                        a.activation(rstd[:, slot:slot + 1], mv[:, slot, 1:2], ACT.Sqrt).then_inc(std_ready, 1)

                    def normalize(m, slot, half):
                        a.wait_ge(norm_ready, m + 1)
                        if not early(m, 2):
                            a.wait_ge(lo_done, m - 1)
                            a.wait_ge(stored_h[slot], 16 * half)
                        for dst in (h_sb[:, slot, :], h16[:, slot, 0:D]):
                            last = a.activation(dst, val[:, slot, :], ACT.Relu, bias=shift[:, slot:slot + 1],
                                                scale=rstd[:, slot:slot + 1])
                        last.then_inc(h_ready, 1)
                    each_tile(a, nothing, both(root, normalize), nothing)

        with ExitStack() as gat:
            sb1, _, _ = opener(gat, "gat")
            key_r = sb1("key_r", [SP_, SB, CH])
            mask_r = sb1("mask_r", [SP_, SB, CH])
            tables(key_r, mask_r)
            weight_scales()
            att_n = sb1("att_n", [TN, NT, 2 * H])
            normalize_x()
            weight_e = sb1("weight_e", [P, NS, 2, 2 * H + 1], f16)
            high_e = sb1("high_e", [P, NS, H])
            with ExitStack() as scores:
                sb2, _, _ = opener(scores, "sco")
                pair_e = sb2("pair_e", [P, NS, 2 * H])
                target_e = sb2("target_e", [P, NS, H])
                edge_attention(pair_e, target_e)
                edge_weights(pair_e, target_e, key_r, mask_r)
            with ExitStack() as sums:
                sb2, _, _ = opener(sums, "sums")
                acc = sb2("acc", [TN, NT, D])
                acc_x = sb2("acc_x", [TN, NT, 2 * H + 1])
                aggregate("gagg", xs_rows, acc, acc_x=acc_x)
                gat_finish(acc, acc_x)
        with ExitStack() as sums:
            acc = opener(sums, "sum0")[0]("acc", [TN, NT, D])
            aggregate("agg0", h_rows, acc, product=(SELF0, b0, None, part0_rows))
            project("neigh0", NEIGH0, h1_rows, acc, part0_rows, split=True, bounded=True)
        with ExitStack() as sums:
            acc = opener(sums, "sum1")[0]("acc", [TN, NT, D])
            aggregate("agg1", h1_rows, acc, product=(SELF1, b1, x1_rows, part1_rows))
            project("neigh1", NEIGH1, out, acc, part1_rows)


_INS = ['x', 'src', 'dst', 'L0_gnn_W', 'L0_gnn_att_src', 'L0_gnn_att_dst', 'L0_gnn_bias',
        'L1_gnn_W_self0', 'L1_gnn_W_neigh0', 'L1_gnn_b0', 'L1_gnn_W_self1', 'L1_gnn_W_neigh1', 'L1_gnn_b1']


def kernel(**inputs):
    import numpy as _np
    import concourse.bacc as _bacc
    from concourse import mybir as _mybir
    from concourse.bass_utils import run_bass_kernel_spmd as _run

    nc = _bacc.Bacc("TRN2", target_bir_lowering=False, num_devices=1)
    arrays, args = {}, []
    for name in _INS:
        a = _np.ascontiguousarray(inputs[name])
        arrays[f"in_{name}_dram"] = a
        args.append(nc.dram_tensor(f"in_{name}_dram", a.shape, _mybir.dt.from_np(a.dtype), kind="ExternalInput").ap())
    out = nc.dram_tensor("out_0_dram", inputs['x'].shape, _mybir.dt.float32, kind="ExternalOutput").ap()
    bass_gat_sage_sage(nc, *args, out)
    r = _run(nc, [arrays], core_ids=[0])
    return r.results[0]["out_0_dram"]
```
